# Optimizing a Trainium2 kernel written in Bass

```python
import numpy as np
import jax
import jax.numpy as jnp

def _softmax(x, axis=-1):
    return jax.nn.softmax(x, axis=axis)

def _gelu(x):
    return jax.nn.gelu(x, approximate=True)

def _silu(x):
    return jax.nn.silu(x)

def _sigmoid(x):
    return jax.nn.sigmoid(x)

def _layernorm(x, axis=-1, eps=1e-05):
    m = jnp.mean(x, axis=axis, keepdims=True)
    v = jnp.var(x, axis=axis, keepdims=True)
    return (x - m) / jnp.sqrt(v + eps)

def _scatter_add(tgt, idx, src, axis=0):
    return tgt.at[idx].add(src)

def _segment_sum(src, seg, n):
    return jax.ops.segment_sum(src, seg, n)
kernel_name = 'mk_perceiver_d1_seqx_r2_7116a6'

def setup_inputs(seed: int=0):
    np.random.seed(seed)
    _w = jnp.asarray

    def _rec_inputs():
        import jax
        import jax.numpy as jnp
        _rk = jax.random.key(seed)
        x = 0.002226 + 0.9996 * jax.random.normal(jax.random.fold_in(_rk, 1), (1, 512, 512), jnp.float32)
        _lenS = 512 - jax.random.randint(jax.random.fold_in(_rk, 7), (1,), 0, max(1, 512 // 4) + 1, jnp.int32)
        _lenS2 = 8192 - jax.random.randint(jax.random.fold_in(_rk, 8), (1,), 0, max(1, 8192 // 4) + 1, jnp.int32)
        _ctx_1024P = jax.random.normal(jax.random.fold_in(_rk, 11), (1, 16, 512), jnp.float32)
        _ctx_1024c = jax.random.dirichlet(jax.random.fold_in(_rk, 511), 0.3 * jnp.ones((16,), jnp.float32), (1, 8192))
        _ctx_1024t = jnp.einsum('bsk,bkd->bsd', _ctx_1024c, _ctx_1024P)
        _ctx_1024t = _ctx_1024t * jax.lax.rsqrt(jnp.mean(jnp.square(_ctx_1024t)) + 1e-12) * 0.953939
        ctx_1024 = -7.10856e-05 + 0.999911 * (_ctx_1024t + 0.3 * jax.random.normal(jax.random.fold_in(_rk, 611), (1, 8192, 512), jnp.float32))
        return (x, ctx_1024)
    x, ctx_1024 = _rec_inputs()

    def _L0_xattn_setup():
        import jax, jax.numpy as jnp
        import numpy as np
        DIM = 512
        HEAD_DIM = 64
        NUM_HEADS = 8
        INNER = HEAD_DIM * NUM_HEADS
        ROT_DIM = HEAD_DIM
        ROPE_BASE = 10000.0
        EPS = 1e-05

        def layer_norm(x, g, b):
            mu = jnp.mean(x, axis=-1, keepdims=True)
            var = jnp.var(x, axis=-1, keepdims=True)
            return (x - mu) * jax.lax.rsqrt(var + EPS) * g + b

        def rope_rotate_k(k):
            n = k.shape[1]
            half = ROT_DIM // 2
            inv_freq = 1.0 / ROPE_BASE ** (jnp.arange(0, ROT_DIM, 2, dtype=jnp.float32) / ROT_DIM)
            theta = jnp.arange(n, dtype=jnp.float32)[:, None] * inv_freq[None, :]
            angles = jnp.concatenate([theta, theta], axis=-1)
            cos = jnp.cos(angles)[None, :, None, :].astype(k.dtype)
            sin = jnp.sin(angles)[None, :, None, :].astype(k.dtype)
            k_rope, k_pass = (k[..., :ROT_DIM], k[..., ROT_DIM:])
            neg_half = jnp.concatenate([-k_rope[..., half:], k_rope[..., :half]], axis=-1)
            k_rope = k_rope * cos + neg_half * sin
            return jnp.concatenate([k_rope, k_pass], axis=-1)
        key = jax.random.key(seed)
        ks = jax.random.split(key, 5)
        b, n, m = (8, 4096, 64)
        s = 1.0 / np.sqrt(DIM)
        return {'x': jax.random.normal(ks[0], (b, n, DIM), jnp.float32), 'latents': jax.random.normal(ks[1], (b, m, DIM), jnp.float32), 'gamma_x': jnp.ones((DIM,), jnp.float32), 'beta_x': jnp.zeros((DIM,), jnp.float32), 'gamma_l': jnp.ones((DIM,), jnp.float32), 'beta_l': jnp.zeros((DIM,), jnp.float32), 'Wq': jax.random.normal(ks[2], (DIM, INNER), jnp.float32) * s, 'Wkv': jax.random.normal(ks[3], (DIM, 2 * INNER), jnp.float32) * s, 'Wo': jax.random.normal(ks[4], (INNER, DIM), jnp.float32) * (1.0 / np.sqrt(INNER))}
    _L0_xattn_all = _L0_xattn_setup()
    _L0_xattn_in = {k: v for k, v in _L0_xattn_all.items() if k in ('gamma_x', 'beta_x', 'gamma_l', 'beta_l', 'Wq', 'Wkv', 'Wo')}
    del _L0_xattn_all

    def _L0_attn_setup():
        import jax, jax.numpy as jnp
        import numpy as np
        N, L, D, A, F, B = (4, 2048, 512, 512, 2048, 8)
        EPS_LN = 1e-06
        EPS_Z = 1e-06

        def _layernorm(x, scale, bias):
            m = jnp.mean(x, axis=-1, keepdims=True)
            v = jnp.mean(jnp.square(x - m), axis=-1, keepdims=True)
            return (x - m) * jax.lax.rsqrt(v + EPS_LN) * scale + bias

        def _block(x, p):
            Wq, bq, Wk, bk, Wv, bv, Wo, bo, ln1_s, ln1_b, Wf1, bf1, Wf2, bf2, ln2_s, ln2_b = p
            residual = x
            q = jnp.einsum('nld,da->nla', x, Wq) + bq
            k = jnp.einsum('nld,da->nla', x, Wk) + bk
            v = jnp.einsum('nld,da->nla', x, Wv) + bv
            Q = jax.nn.elu(q) + 1.0
            K = jax.nn.elu(k) + 1.0
            KV = jnp.einsum('nsh,nsh->nh', K, v)
            Ksum = jnp.sum(K, axis=1)
            Z = 1.0 / (Q * Ksum[:, None, :] + EPS_Z)
            V = Q * KV[:, None, :] * Z
            attn = jax.nn.gelu(jnp.einsum('nla,ad->nld', V, Wo) + bo)
            x = _layernorm(attn + residual, ln1_s, ln1_b)
            residual = x
            h = jax.nn.gelu(jnp.einsum('nld,df->nlf', x, Wf1) + bf1)
            ff = jax.nn.gelu(jnp.einsum('nlf,fd->nld', h, Wf2) + bf2)
            x = _layernorm(ff + residual, ln2_s, ln2_b)
            return (x, None)
        key = jax.random.key(seed)
        ks = jax.random.split(key, 10)
        s = 0.02
        x = jax.random.normal(ks[0], (N, L, D), dtype=jnp.float32)
        Wq = jax.random.normal(ks[1], (B, D, A), dtype=jnp.float32) * s
        Wk = jax.random.normal(ks[2], (B, D, A), dtype=jnp.float32) * s
        Wv = jax.random.normal(ks[3], (B, D, A), dtype=jnp.float32) * s
        Wo = jax.random.normal(ks[4], (B, A, D), dtype=jnp.float32) * s
        Wf1 = jax.random.normal(ks[5], (B, D, F), dtype=jnp.float32) * s
        Wf2 = jax.random.normal(ks[6], (B, F, D), dtype=jnp.float32) * s
        return {'x': x, 'Wq': Wq, 'bq': jnp.zeros((B, A), jnp.float32), 'Wk': Wk, 'bk': jnp.zeros((B, A), jnp.float32), 'Wv': Wv, 'bv': jnp.zeros((B, A), jnp.float32), 'Wo': Wo, 'bo': jnp.zeros((B, D), jnp.float32), 'ln1_s': jnp.ones((B, D), jnp.float32), 'ln1_b': jnp.zeros((B, D), jnp.float32), 'Wf1': Wf1, 'bf1': jnp.zeros((B, F), jnp.float32), 'Wf2': Wf2, 'bf2': jnp.zeros((B, D), jnp.float32), 'ln2_s': jnp.ones((B, D), jnp.float32), 'ln2_b': jnp.zeros((B, D), jnp.float32)}
    _L0_attn_all = _L0_attn_setup()
    _L0_attn_in = {k: v for k, v in _L0_attn_all.items() if k in ('Wq', 'bq', 'Wk', 'bk', 'Wv', 'bv', 'Wo', 'bo', 'ln1_s', 'ln1_b', 'Wf1', 'bf1', 'Wf2', 'bf2', 'ln2_s', 'ln2_b')}
    del _L0_attn_all

    def _L0_ffn_setup():
        import jax, jax.numpy as jnp
        import numpy as np
        DM, NE, ES, ESZ = (512, 16, 4, 64)
        BATCH, SEQ = (8, 1024)
        key = jax.random.key(seed)
        k = jax.random.split(key, 5)
        scale = 0.02
        return {'x': jax.random.normal(k[0], (BATCH, SEQ, DM), dtype=jnp.float32), 'controller': jax.random.normal(k[1], (DM, NE, ES), dtype=jnp.float32) * scale, 'f1': jax.random.normal(k[2], (DM, NE, ES, ESZ), dtype=jnp.float32) * scale, 'f2': jax.random.normal(k[3], (NE, ES, ESZ, DM), dtype=jnp.float32) * scale, 'bias': jax.random.normal(k[4], (NE, ES, ESZ), dtype=jnp.float32) * scale}
    _L0_ffn_all = _L0_ffn_setup()
    _L0_ffn_in = {k: v for k, v in _L0_ffn_all.items() if k in ('controller', 'f1', 'f2', 'bias')}
    del _L0_ffn_all
    return {'x': x, 'ctx_1024': ctx_1024, 'L0_xattn_gamma_x': _L0_xattn_in['gamma_x'], 'L0_xattn_beta_x': _L0_xattn_in['beta_x'], 'L0_xattn_gamma_l': _L0_xattn_in['gamma_l'], 'L0_xattn_beta_l': _L0_xattn_in['beta_l'], 'L0_xattn_Wq': _L0_xattn_in['Wq'], 'L0_xattn_Wkv': _L0_xattn_in['Wkv'], 'L0_xattn_Wo': _L0_xattn_in['Wo'], 'L0_attn_Wq': _L0_attn_in['Wq'], 'L0_attn_bq': _L0_attn_in['bq'], 'L0_attn_Wk': _L0_attn_in['Wk'], 'L0_attn_bk': _L0_attn_in['bk'], 'L0_attn_Wv': _L0_attn_in['Wv'], 'L0_attn_bv': _L0_attn_in['bv'], 'L0_attn_Wo': _L0_attn_in['Wo'], 'L0_attn_bo': _L0_attn_in['bo'], 'L0_attn_ln1_s': _L0_attn_in['ln1_s'], 'L0_attn_ln1_b': _L0_attn_in['ln1_b'], 'L0_attn_Wf1': _L0_attn_in['Wf1'], 'L0_attn_bf1': _L0_attn_in['bf1'], 'L0_attn_Wf2': _L0_attn_in['Wf2'], 'L0_attn_bf2': _L0_attn_in['bf2'], 'L0_attn_ln2_s': _L0_attn_in['ln2_s'], 'L0_attn_ln2_b': _L0_attn_in['ln2_b'], 'L0_ffn_controller': _L0_ffn_in['controller'], 'L0_ffn_f1': _L0_ffn_in['f1'], 'L0_ffn_f2': _L0_ffn_in['f2'], 'L0_ffn_bias': _L0_ffn_in['bias']}

def reference(x, ctx_1024, L0_xattn_gamma_x, L0_xattn_beta_x, L0_xattn_gamma_l, L0_xattn_beta_l, L0_xattn_Wq, L0_xattn_Wkv, L0_xattn_Wo, L0_attn_Wq, L0_attn_bq, L0_attn_Wk, L0_attn_bk, L0_attn_Wv, L0_attn_bv, L0_attn_Wo, L0_attn_bo, L0_attn_ln1_s, L0_attn_ln1_b, L0_attn_Wf1, L0_attn_bf1, L0_attn_Wf2, L0_attn_bf2, L0_attn_ln2_s, L0_attn_ln2_b, L0_ffn_controller, L0_ffn_f1, L0_ffn_f2, L0_ffn_bias):
    import jax
    import jax.numpy as jnp

    def _L0_xattn_ref(x, latents, gamma_x, beta_x, gamma_l, beta_l, Wq, Wkv, Wo):
        import jax, jax.numpy as jnp
        import numpy as np
        DIM = 512
        HEAD_DIM = 64
        NUM_HEADS = 8
        INNER = HEAD_DIM * NUM_HEADS
        ROT_DIM = HEAD_DIM
        ROPE_BASE = 10000.0
        EPS = 1e-05

        def layer_norm(x, g, b):
            mu = jnp.mean(x, axis=-1, keepdims=True)
            var = jnp.var(x, axis=-1, keepdims=True)
            return (x - mu) * jax.lax.rsqrt(var + EPS) * g + b

        def rope_rotate_k(k):
            n = k.shape[1]
            half = ROT_DIM // 2
            inv_freq = 1.0 / ROPE_BASE ** (jnp.arange(0, ROT_DIM, 2, dtype=jnp.float32) / ROT_DIM)
            theta = jnp.arange(n, dtype=jnp.float32)[:, None] * inv_freq[None, :]
            angles = jnp.concatenate([theta, theta], axis=-1)
            cos = jnp.cos(angles)[None, :, None, :].astype(k.dtype)
            sin = jnp.sin(angles)[None, :, None, :].astype(k.dtype)
            k_rope, k_pass = (k[..., :ROT_DIM], k[..., ROT_DIM:])
            neg_half = jnp.concatenate([-k_rope[..., half:], k_rope[..., :half]], axis=-1)
            k_rope = k_rope * cos + neg_half * sin
            return jnp.concatenate([k_rope, k_pass], axis=-1)
        b, n, _ = x.shape
        m = latents.shape[1]
        h, d = (NUM_HEADS, HEAD_DIM)
        scale = d ** (-0.5)
        xn = layer_norm(x, gamma_x, beta_x)
        ln = layer_norm(latents, gamma_l, beta_l)
        q = (ln @ Wq).reshape(b, m, h, d)
        kv_x = xn @ Wkv
        k_x, v_x = (kv_x[..., :INNER], kv_x[..., INNER:])
        kv_l = ln @ Wkv
        k_l, v_l = (kv_l[..., :INNER], kv_l[..., INNER:])
        k_x = k_x.reshape(b, n, h, d)
        v_x = v_x.reshape(b, n, h, d)
        k_x = rope_rotate_k(k_x)
        q = jnp.transpose(q, (0, 2, 1, 3)) * scale
        k_x = jnp.transpose(k_x, (0, 2, 1, 3))
        v_x = jnp.transpose(v_x, (0, 2, 1, 3))
        k_l = jnp.transpose(k_l.reshape(b, m, h, d), (0, 2, 1, 3))
        v_l = jnp.transpose(v_l.reshape(b, m, h, d), (0, 2, 1, 3))
        k = jnp.concatenate([k_x, k_l], axis=2)
        v = jnp.concatenate([v_x, v_l], axis=2)
        sim = jnp.einsum('bhid,bhjd->bhij', q, k)
        attn = jax.nn.softmax(sim, axis=-1)
        out = jnp.einsum('bhij,bhjd->bhid', attn, v)
        out = jnp.transpose(out, (0, 2, 1, 3)).reshape(b, m, INNER)
        return out @ Wo

    def _L0_attn_ref(x, Wq, bq, Wk, bk, Wv, bv, Wo, bo, ln1_s, ln1_b, Wf1, bf1, Wf2, bf2, ln2_s, ln2_b):
        import jax, jax.numpy as jnp
        import numpy as np
        N, L, D, A, F, B = (4, 2048, 512, 512, 2048, 8)
        EPS_LN = 1e-06
        EPS_Z = 1e-06

        def _layernorm(x, scale, bias):
            m = jnp.mean(x, axis=-1, keepdims=True)
            v = jnp.mean(jnp.square(x - m), axis=-1, keepdims=True)
            return (x - m) * jax.lax.rsqrt(v + EPS_LN) * scale + bias

        def _block(x, p):
            Wq, bq, Wk, bk, Wv, bv, Wo, bo, ln1_s, ln1_b, Wf1, bf1, Wf2, bf2, ln2_s, ln2_b = p
            residual = x
            q = jnp.einsum('nld,da->nla', x, Wq) + bq
            k = jnp.einsum('nld,da->nla', x, Wk) + bk
            v = jnp.einsum('nld,da->nla', x, Wv) + bv
            Q = jax.nn.elu(q) + 1.0
            K = jax.nn.elu(k) + 1.0
            KV = jnp.einsum('nsh,nsh->nh', K, v)
            Ksum = jnp.sum(K, axis=1)
            Z = 1.0 / (Q * Ksum[:, None, :] + EPS_Z)
            V = Q * KV[:, None, :] * Z
            attn = jax.nn.gelu(jnp.einsum('nla,ad->nld', V, Wo) + bo)
            x = _layernorm(attn + residual, ln1_s, ln1_b)
            residual = x
            h = jax.nn.gelu(jnp.einsum('nld,df->nlf', x, Wf1) + bf1)
            ff = jax.nn.gelu(jnp.einsum('nlf,fd->nld', h, Wf2) + bf2)
            x = _layernorm(ff + residual, ln2_s, ln2_b)
            return (x, None)
        params = (Wq, bq, Wk, bk, Wv, bv, Wo, bo, ln1_s, ln1_b, Wf1, bf1, Wf2, bf2, ln2_s, ln2_b)
        out, _ = jax.lax.scan(_block, x, params)
        return out

    def _L0_ffn_ref(x, controller, f1, f2, bias):
        import jax, jax.numpy as jnp
        import numpy as np
        DM, NE, ES, ESZ = (512, 16, 4, 64)
        BATCH, SEQ = (8, 1024)
        ne = controller.shape[1]
        d = x.shape[-1]
        grouped = x.reshape(x.shape[:-2] + (-1, ne, d))
        logits = jnp.einsum('...btd,des->...btes', grouped, controller)
        tie = jnp.linspace(0.0, 1e-06, ne, dtype=logits.dtype).reshape(ne, 1, 1)
        logits = logits + tie
        perm = (logits == jnp.max(logits, axis=-3, keepdims=True)).astype(x.dtype)
        sel = jnp.einsum('...btd,...btes->...besd', grouped, perm)
        inner = jax.nn.relu(jnp.einsum('...besd,desf->...besf', sel, f1) + bias)
        inter = jnp.einsum('...besf,esfd->...besd', inner, f2)
        out = jnp.einsum('...besd,...btes->...btd', inter, perm)
        return out.reshape(x.shape)
    x = x + _L0_xattn_ref(ctx_1024, _layernorm(x, axis=-1), L0_xattn_gamma_x, L0_xattn_beta_x, L0_xattn_gamma_l, L0_xattn_beta_l, L0_xattn_Wq, L0_xattn_Wkv, L0_xattn_Wo)
    x = x + _L0_attn_ref(_layernorm(x, axis=-1), L0_attn_Wq, L0_attn_bq, L0_attn_Wk, L0_attn_bk, L0_attn_Wv, L0_attn_bv, L0_attn_Wo, L0_attn_bo, L0_attn_ln1_s, L0_attn_ln1_b, L0_attn_Wf1, L0_attn_bf1, L0_attn_Wf2, L0_attn_bf2, L0_attn_ln2_s, L0_attn_ln2_b)
    x = x + _L0_ffn_ref(_layernorm(x, axis=-1), L0_ffn_controller, L0_ffn_f1, L0_ffn_f2, L0_ffn_bias)
    return x

_drawn_inputs = setup_inputs


def setup_inputs(seed=0):
    import zlib

    import numpy as np

    out = dict(_drawn_inputs(seed))
    spreads = {'L0_xattn_gamma_x': (1.0, 0.2),
     'L0_xattn_beta_x': (0.0, 0.1),
     'L0_xattn_gamma_l': (1.0, 0.6),
     'L0_xattn_beta_l': (0.0, 0.732),
     'L0_attn_bq': (0.0, 2.0),
     'L0_attn_bk': (0.0, 2.0),
     'L0_attn_bv': (0.0, 0.1),
     'L0_attn_bo': (0.0, 0.1),
     'L0_attn_ln1_s': (1.0, 0.2),
     'L0_attn_ln1_b': (0.0, 0.1),
     'L0_attn_bf1': (0.0, 0.1),
     'L0_attn_bf2': (0.0, 0.1),
     'L0_attn_ln2_s': (1.0, 0.2),
     'L0_attn_ln2_b': (0.0, 0.1)}
    factors = {'L0_attn_Wq': 64.0, 'L0_attn_Wk': 32.487, 'L0_ffn_bias': 25.947}
    for name, (base, spread) in spreads.items():
        noise = np.random.default_rng([zlib.crc32(name.encode()), seed]).standard_normal(out[name].shape)
        drawn = base * np.exp(spread * noise) if base else spread * noise
        out[name] = jnp.asarray(drawn.astype(out[name].dtype))
    for name, factor in factors.items():
        out[name] = (out[name] * factor).astype(out[name].dtype)
    return out
```

```python
from contextlib import ExitStack

import numpy as np

import concourse.bass as bass
from concourse import mybir

F32 = mybir.dt.float32
F16 = mybir.dt.float16
BF16 = mybir.dt.bfloat16
ALU = mybir.AluOpType
ACT = mybir.ActivationFunctionType
AX_X = mybir.AxisListType.X

P = 128
TOK = 512
D = 512
TT = TOK // P
CH = D // P
HD = 64
PAIRS = D // (2 * HD)
CTX = 8192
BLK = 512
CTX_BLOCKS = CTX // BLK
KB = CTX_BLOCKS + TOK // BLK
SUB = BLK // P
BLOCKS = PAIRS * KB
EPS_OUTER = 1e-5
EPS_XATTN = 1e-5
CHUNKS = 12
F2, KQVO, F1 = 0, 4, 8
XWO = 3
UNITS = 2 * TT
STAGES = 3
PIECES = 4 * STAGES
M_UNIT = 256.0


class Kernel:
    pass


def slots(w, first, count, dtype, width):
    flat = w[:, first:first + count].rearrange("p a c n -> p (a c n)")
    if dtype != w.dtype:
        flat = flat.bitcast(dtype)
    return flat.rearrange("p (c n) -> p c n", n=width)


def rows(w, first, count):
    return w[:, first:first + count].rearrange("p a n -> p (a n)").bitcast(F32)


def product3(pe, out, lhs, rhs, first, last, **kw):
    (lh, ll), (rh, rl) = lhs, rhs
    pe.matmul(out, lh, rh, start=first, stop=False, **kw)
    pe.matmul(out, lh, rl, start=False, stop=False, **kw)
    return pe.matmul(out, ll, rh, start=False, stop=last, **kw)


def latents_phase(k):
    nc = k.nc
    sems = []
    with ExitStack() as ctx:
        def sb(name, shape, dt):
            return ctx.enter_context(nc.sbuf_tensor(name, shape, dt))

        def sem(name):
            sems.append(nc.alloc_semaphore(name))
            return sems[-1]

        wkv = slots(k.wt_hi, 4, 4, F32, 2 * D)
        wkv_g = slots(k.wt_hi, 8, 4, F32, 2 * D)
        wkv_hi = slots(k.wt_lo, 4, 2, F16, 2 * D)
        wkv_lo = slots(k.wt_lo, 2, 2, BF16, 2 * D)
        wq, z = (rows(k.h_lo, 8 * n, 8).rearrange("p (c n) -> p c n", n=D) for n in range(2))
        lat_t = slots(k.wt_lo, 6, 2, F32, D)
        raw, xn = [k.stage[:, u] for u in range(2)], k.stage[:, 2]
        wq_hi = sb("wq_hi", [P, CH, D], F16)
        wq_lo = sb("wq_lo", [P, CH, D], BF16)
        vecs = sb("vecs", [P, 4, CH], F32)
        beta_cols = sb("beta_cols", [P, CH, P], F32)
        stats = sb("stats", [P, TT, 6], F32)
        mv = sb("mv", [P, TT, 2], F32)
        var_eps = sb("var_eps", [P, TT], F32)
        rstd = sb("rstd", [P, TT], F32)
        lat_hi = sb("lat_hi", [P, CH, TOK], F16)
        lat_lo = sb("lat_lo", [P, CH, TOK], BF16)
        kt_hi, kt_lo = k.kt[1][:, 0], k.kt[1][:, 1]
        v_out = sb("v_out", [P, PAIRS, SUB, P], F32)
        tp = [ctx.enter_context(nc.psum_tensor(f"tp{i}", [P, TOK], F32)) for i in range(2)]
        mm = [ctx.enter_context(nc.psum_tensor(f"mm{i}", [P, 512], F32)) for i in range(4)]

        x_in = [sem(f"x_in{t}") for t in range(TT)]
        w_in, vec_in, raw_in = sem("w_in"), sem("vec_in"), sem("raw_in")
        zeroed, consts = sem("zeroed"), sem("consts")
        stats_done, mv_done, var_done, rstd_done, norm_done = (sem(n) for n in (
            "stats_done", "mv_done", "var_done", "rstd_done", "norm_done"))
        tp_ready, lat_done, lat_hi_done, lat_lo_done = (sem(n) for n in (
            "tp_ready", "lat_done", "lat_hi_done", "lat_lo_done"))
        w_hi_done, w_lo_done, w_scaled, wg_hi_done, wg_lo_done, beta_done = (sem(n) for n in (
            "w_hi_done", "w_lo_done", "w_scaled", "wg_hi_done", "wg_lo_done", "beta_done"))
        mm_ready, hi_copied, lo_copied, v_copied, stored = (sem(n) for n in (
            "mm_ready", "hi_copied", "lo_copied", "v_copied", "stored"))

        with nc.Block() as block:
            @block.sync
            def _(sp):
                for t in range(TT):
                    sp.dma_start(k.x_sb[:, t, :], k.x[t * P:(t + 1) * P, :]).then_inc(x_in[t], 16)
                for n, v in enumerate((k.gamma_x, k.beta_x, k.gamma_l, k.beta_l)):
                    sp.dma_start(vecs[:, n, :], v.rearrange("(c p) -> p c", p=P),
                                 allow_slow_non_contiguous=True).then_inc(vec_in, 16)
                sp.dma_start(wq, k.wq.rearrange("(c p) n -> p c n", p=P)).then_inc(w_in, 16)
                sp.dma_start(wkv, k.wkv.rearrange("(c p) n -> p c n", p=P)).then_inc(w_in, 16)
                for b in range(2):
                    sp.dma_start(raw[b], k.ctx.rearrange("(b t p) d -> b p t d", p=P, t=SUB)[b]).then_inc(raw_in, 16)
                sp.wait_ge(hi_copied, 4 * PAIRS + PAIRS)
                sp.dma_start(k.k_store(0, CTX_BLOCKS), kt_hi).then_inc(stored, 16)
                sp.wait_ge(lo_copied, 2 * PAIRS + PAIRS)
                sp.dma_start(k.k_store(1, CTX_BLOCKS), kt_lo).then_inc(stored, 16)
                sp.wait_ge(v_copied, TT)
                sp.dma_start(k.v_store(CTX_BLOCKS), v_out[:]).then_inc(stored, 16)
                sp.wait_ge(stored, 48)
                sp.wait_ge(raw_in, 32)

            @block.gpsimd
            def _(pool):
                g = nc.gpsimd
                g.memset(k.ident[:], 0.0).then_inc(zeroed, 1)
                g.memset(k.ident16[:], 0.0).then_inc(zeroed, 1)
                g.memset(k.neg_half[:], -0.5).then_inc(consts, 1)
                g.memset(k.ones[:], 1.0).then_inc(consts, 1)
                pool.wait_ge(zeroed, 2)
                for m in (k.ident, k.ident16):
                    g.affine_select(out=m[:], in_=m[:], compare_op=ALU.not_equal, fill=1.0, base=0,
                                    pattern=[[-1, P]], channel_multiplier=1).then_inc(consts, 1)
                pool.wait_ge(consts, 4)
                for n in range(3):
                    pool.wait_ge(var_done, n + 1)
                    g.tensor_tensor(rstd[:], var_eps[:], k.neg_half[:, 0:TT], ALU.pow).then_inc(rstd_done, 1)

            @block.vector
            def _(dve):
                v = nc.vector

                def norm(n, src, dst, eps):
                    for t in range(TT):
                        if n == 0:
                            dve.wait_ge(x_in[t], 16)
                        if n == 1:
                            dve.wait_ge(norm_done, t + 1)
                        v.bn_stats(stats[:, t, :], src[:, t, :]).then_inc(stats_done, 1)
                    dve.wait_ge(stats_done, TT * (n + 1))
                    for t in range(TT):
                        v.bn_aggr(mv[:, t, :], stats[:, t, :]).then_inc(mv_done, 1)
                    dve.wait_ge(mv_done, TT * (n + 1))
                    v.tensor_scalar(var_eps[:], mv[:, :, 1], eps, None, ALU.add).then_inc(var_done, 1)
                    dve.wait_ge(rstd_done, n + 1)
                    for t in range(TT):
                        v.tensor_scalar(dst[:, t, :], src[:, t, :], mv[:, t, 0:1], rstd[:, t:t + 1],
                                        ALU.subtract, ALU.mult).then_inc(norm_done, 1)

                norm(0, k.x_sb, z, EPS_OUTER)
                norm(1, z, z, EPS_XATTN)
                dve.wait_ge(w_in, 32)
                dve.wait_ge(w_hi_done, 1)
                v.tensor_tensor(wq_lo[:], wq, wq_hi[:], ALU.subtract).then_inc(w_lo_done, 1)
                dve.wait_ge(vec_in, 64)
                for c in range(CH):
                    dve.wait_ge(tp_ready, c + 1)
                    v.tensor_scalar(lat_t[:, c, :], tp[c % 2][:], vecs[:, 2, c:c + 1], vecs[:, 3, c:c + 1],
                                    ALU.mult, ALU.add).then_inc(lat_done, 1)
                for c in range(CH):
                    dve.wait_ge(lat_hi_done, c + 1)
                    v.tensor_tensor(lat_lo[:, c, :], lat_t[:, c, :], lat_hi[:, c, :],
                                    ALU.subtract).then_inc(lat_lo_done, 1)
                dve.wait_ge(w_hi_done, 2)
                v.tensor_tensor(wkv_lo, wkv, wkv_hi, ALU.subtract).then_inc(w_lo_done, 1)
                for c in range(CH):
                    v.tensor_scalar(wkv_g[:, c, :], wkv[:, c, :], vecs[:, 0, c:c + 1], None,
                                    ALU.mult).then_inc(w_scaled, 1)
                    v.tensor_scalar(beta_cols[:, c, :], k.ones[:], vecs[:, 1, c:c + 1], None,
                                    ALU.mult).then_inc(beta_done, 1)
                for p in range(PAIRS):
                    dve.wait_ge(mm_ready, p + 1)
                    dve.wait_ge(hi_copied, 4 * (p + 1))
                    for s in range(2):
                        rows = slice(HD * s, HD * (s + 1))
                        v.scalar_tensor_tensor(out=k.q_lo[0:HD, 2 * p + s, :], in0=mm[p % 4][rows, :],
                                               scalar=HD ** -0.5, in1=k.q_hi[rows, 2 * p + s, :],
                                               op0=ALU.mult, op1=ALU.subtract).then_inc(lo_copied, 1)
                for p in range(PAIRS):
                    dve.wait_ge(hi_copied, 4 * PAIRS + p + 1)
                    v.tensor_tensor(kt_lo[:, p, :], mm[p % 4][:], kt_hi[:, p, :],
                                    ALU.subtract).then_inc(lo_copied, 1)
                for c in range(CH):
                    dve.wait_ge(wg_hi_done, c + 1)
                    v.tensor_tensor(k.wg_lo[:, c, :], wkv_g[:, c, :], k.wg_hi[:, c, :],
                                    ALU.subtract).then_inc(wg_lo_done, 1)
                dve.wait_ge(raw_in, 32)
                norm(2, raw[0], xn, EPS_XATTN)

            @block.scalar
            def _(act):
                a = nc.scalar
                act.wait_ge(w_in, 32)
                a.activation(wq_hi[:], wq, ACT.Copy).then_inc(w_hi_done, 1)
                a.activation(wkv_hi, wkv, ACT.Copy).then_inc(w_hi_done, 1)
                for c in range(CH):
                    act.wait_ge(lat_done, c + 1)
                    a.activation(lat_hi[:, c, :], lat_t[:, c, :], ACT.Copy).then_inc(lat_hi_done, 1)
                for p in range(PAIRS):
                    act.wait_ge(mm_ready, p + 1)
                    for s in range(2):
                        for half in range(2):
                            a.activation(k.q_hi[HD * half:HD * (half + 1), 2 * p + s, :],
                                         mm[p % 4][HD * s:HD * (s + 1), :], ACT.Copy,
                                         scale=HD ** -0.5).then_inc(hi_copied, 1)
                for p in range(PAIRS):
                    act.wait_ge(mm_ready, PAIRS + p + 1)
                    a.activation(kt_hi[:, p, :], mm[p % 4][:], ACT.Copy).then_inc(hi_copied, 1)
                    act.wait_ge(w_scaled, p + 1)
                    a.activation(k.wg_hi[:, p, :], wkv_g[:, p, :], ACT.Copy).then_inc(wg_hi_done, 1)
                for t in range(TT):
                    act.wait_ge(mm_ready, 2 * PAIRS + t + 1)
                    a.activation(v_out[:, :, t, :], mm[t % 4][:].rearrange("p (a d) -> p a d", a=PAIRS),
                                 ACT.Copy).then_inc(v_copied, 1)
                for n in range(2):
                    act.wait_ge(mm_ready, 2 * PAIRS + TT + n + 1)
                    a.activation(k.kv_bias[:, n * D:(n + 1) * D], mm[n][:], ACT.Copy).then_inc(v_copied, 1)

            @block.tensor
            def _(pe):
                t_ = nc.tensor
                pe.wait_ge(consts, 4)
                pe.wait_ge(norm_done, 2 * TT)
                for c in range(CH):
                    if c >= 2:
                        pe.wait_ge(lat_done, c - 1)
                    for t in range(TT):
                        m = t_.transpose(tp[c % 2][:, t * P:(t + 1) * P], z[:, t, c * P:(c + 1) * P], k.ident[:])
                    m.then_inc(tp_ready, 1)
                pe.wait_ge(lat_lo_done, CH)
                pe.wait_ge(w_lo_done, 1)
                for p in range(PAIRS):
                    for c in range(CH):
                        cols = slice(p * P, (p + 1) * P)
                        m = product3(t_, mm[p % 4][:], (wq_hi[:, c, cols], wq_lo[:, c, cols]),
                                     (lat_hi[:, c, :], lat_lo[:, c, :]), c == 0, c == CH - 1)
                    m.then_inc(mm_ready, 1)
                pe.wait_ge(w_lo_done, 2)
                for p in range(PAIRS):
                    pe.wait_ge(lo_copied, 2 * (p + 1))
                    for c in range(CH):
                        cols = slice(p * P, (p + 1) * P)
                        m = product3(t_, mm[p % 4][:], (wkv_hi[:, c, cols], wkv_lo[:, c, cols]),
                                     (lat_hi[:, c, :], lat_lo[:, c, :]), c == 0, c == CH - 1)
                    m.then_inc(mm_ready, 1)
                for t in range(TT):
                    pe.wait_ge(lo_copied, 2 * PAIRS + t + 1)
                    for c in range(CH):
                        rows = slice(t * P, (t + 1) * P)
                        m = product3(t_, mm[t % 4][:], (lat_hi[:, c, rows], lat_lo[:, c, rows]),
                                     (wkv_hi[:, c, D:], wkv_lo[:, c, D:]), c == 0, c == CH - 1)
                    m.then_inc(mm_ready, 1)
                pe.wait_ge(beta_done, CH)
                for n in range(2):
                    pe.wait_ge(v_copied, n + 1)
                    for c in range(CH):
                        m = t_.matmul(mm[n][:], beta_cols[:, c, :], wkv[:, c, n * D:(n + 1) * D],
                                      start=c == 0, stop=c == CH - 1)
                    m.then_inc(mm_ready, 1)
    k.spare_semaphores = sems


def context_phase(k):
    nc = k.nc
    with ExitStack() as ctx:
        def sb(name, shape, dt):
            return ctx.enter_context(nc.sbuf_tensor(name, shape, dt))

        def sem(name):
            return ctx.enter_context(nc.semaphore(name))

        def pb(name, shape, dt):
            return ctx.enter_context(nc.psum_tensor(name, shape, dt))

        raw, xn = [k.stage[:, u] for u in range(2)], k.stage[:, 2]
        tab = [sb(f"tab{u}", [P, SUB, HD], F32) for u in range(2)]
        stats = sb("c_stats", [P, SUB, 6], F32)
        mv = sb("c_mv", [P, SUB, 2], F32)
        var_eps = sb("c_var_eps", [P, SUB], F32)
        rstd = sb("c_rstd", [P, SUB], F32)
        xt_hi = [sb(f"xt_hi{u}", [P, CH, BLK], F16) for u in range(2)]
        xt_lo = [sb(f"xt_lo{u}", [P, CH, BLK], BF16) for u in range(2)]
        kf = [rows(k.h_lo, 2 * n, 2) for n in range(2)]
        k_cos = [sb(f"k_cos{n}", [P, D], F32) for n in range(2)]
        k_sin = [sb(f"k_sin{n}", [P, D], F32) for n in range(2)]
        kr = [sb(f"kr{n}", [P, D], F32) for n in range(2)]
        kr_hi = [sb(f"kr_hi{n}", [P, D], F16) for n in range(2)]
        kr_lo = [sb(f"kr_lo{n}", [P, D], F16) for n in range(2)]
        kt = k.kt
        vo = [slots(k.wt_lo, 2 + 2 * u, 2, F32, D).rearrange("p a (t d) -> p a t d", d=P) for u in range(2)]
        tp = [pb(f"c_tp{n}", [P, BLK], F32) for n in range(2)]
        kp = [pb(f"c_kp{n}", [P, D], F32) for n in range(2)]
        vp = pb("c_vp", [P, D], F32)
        mx = pb("c_mx", [P, BLK], F32)
        ktp = [pb(f"c_ktp{n}", [P, 2, PAIRS, P], F16) for n in range(2)]

        loaded = [sem(f"c_loaded{u}") for u in range(2)]
        stored = [sem(f"c_stored{u}") for u in range(2)]
        stats_done, mv_done, var_done, rstd_done, norm_done = (sem(n) for n in (
            "c_stats_done", "c_mv_done", "c_var_done", "c_rstd_done", "c_norm_done"))
        tp_ready, xt_hi_done, xt_lo_done = (sem(n) for n in ("c_tp_ready", "xt_hi_done", "xt_lo_done"))
        k_ready, k_biased, k_mult, k_added, k_hi_done, k_lo_done = (sem(n) for n in (
            "k_ready", "k_biased", "k_mult", "k_added", "k_hi_done", "k_lo_done"))
        ktp_ready, kt_copied, v_ready, v_copied = (sem(n) for n in (
            "ktp_ready", "kt_copied", "v_ready", "c_v_copied"))

        mx_ready, mx_done = sem("c_mx_ready"), sem("c_mx_done")
        passed = sem("c_passed")

        ctx_v = k.ctx.rearrange("(b t p) d -> b p t d", p=P, t=SUB)
        tab_v = k.rope.rearrange("p (b t) f -> b p t f", t=SUB)
        PAIRS_OF_BLOCKS = CTX_BLOCKS // 2

        def over_blocks(eng, body):
            for u in range(2):
                body(0, u)
            with eng.Fori(1, PAIRS_OF_BLOCKS - 1) as i:
                for u in range(2):
                    body(i, u)
            for u in range(2):
                body(PAIRS_OF_BLOCKS - 1, u)

        def is_first(i):
            return isinstance(i, int) and i == 0

        def is_last(i, u):
            return isinstance(i, int) and i == PAIRS_OF_BLOCKS - 1 and u == 1

        def succ(i, u):
            return (i, 1) if u == 0 else (i + 1, 0)

        with nc.Block() as block:
            @block.sync
            def _(sp):
                def load(i, u):
                    b = 2 * i + u
                    if is_first(i):
                        sp.sem_inc(loaded[u], 16)
                    else:
                        sp.dma_start(raw[u], ctx_v[b]).then_inc(loaded[u], 16)
                    sp.dma_start(tab[u][:], tab_v[b]).then_inc(loaded[u], 16)

                load(0, 0)
                load(0, 1)

                def body(i, u):
                    b = 2 * i + u
                    if not (isinstance(i, int) and i == PAIRS_OF_BLOCKS - 1):
                        sp.wait_ge(norm_done, SUB * b + SUB)
                        sp.sem_inc(passed, 1)
                        sp.wait_ge(k_mult, 3 * (SUB * b + SUB))
                        sp.sem_inc(passed, 1)
                        load(i + 1, u)
                    sp.wait_ge(kt_copied, SUB * b + SUB)
                    sp.sem_inc(passed, 1)
                    for hl in range(2):
                        sp.dma_start(k.k_store(hl, b), kt[u][:, hl]).then_inc(stored[u], 16)
                    sp.wait_ge(v_copied, SUB * b + SUB)
                    sp.sem_inc(passed, 1)
                    sp.dma_start(k.v_store(b), vo[u]).then_inc(stored[u], 16)

                over_blocks(sp, body)
                for u in range(2):
                    sp.wait_ge(stored[u], 48 * PAIRS_OF_BLOCKS)

            @block.gpsimd
            def _(pool):
                g = nc.gpsimd

                def rstd_of(i, u):
                    b = 2 * i + u
                    pool.wait_ge(var_done, b + 1)
                    g.tensor_tensor(rstd[:], var_eps[:], k.neg_half[:, 0:SUB], ALU.pow).then_inc(rstd_done, 1)

                pool.sem_inc(rstd_done, 1)

                def body(i, u):
                    b = 2 * i + u
                    if not is_last(i, u):
                        rstd_of(*succ(i, u))
                    for t in range(SUB):
                        n, r = SUB * b + t, t % 2
                        pool.wait_ge(k_mult, 3 * n + 3)
                        if not (is_first(i) and u == 0 and t < 2):
                            pool.wait_ge(k_hi_done, n - 1)
                            pool.wait_ge(k_lo_done, n - 1)
                        g.tensor_tensor(kr[r][:], k_cos[r][:], k_sin[r][:], ALU.add).then_inc(k_added, 1)
                        pool.wait_ge(k_hi_done, n + 1)
                        if not (is_first(i) and u == 0 and t < 2):
                            pool.wait_ge(ktp_ready, n - 1)
                        g.tensor_tensor(kr_lo[r][:], kr[r][:], kr_hi[r][:], ALU.subtract).then_inc(k_lo_done, 1)

                over_blocks(pool, body)

            @block.vector
            def _(dve):
                v = nc.vector

                def norm_stats(i, u):
                    b = 2 * i + u
                    dve.wait_ge(loaded[u], 32 * (i + 1))
                    for t in range(SUB):
                        v.bn_stats(stats[:, t, :], raw[u][:, t, :]).then_inc(stats_done, 1)
                    dve.wait_ge(stats_done, SUB * b + SUB)
                    dve.sem_inc(passed, 1)
                    for t in range(SUB):
                        v.bn_aggr(mv[:, t, :], stats[:, t, :]).then_inc(mv_done, 1)
                    dve.wait_ge(mv_done, SUB * b + SUB)
                    v.tensor_scalar(var_eps[:], mv[:, :, 1], EPS_XATTN, None, ALU.add).then_inc(var_done, 1)

                def normalise(i, u):
                    b = 2 * i + u
                    dve.wait_ge(rstd_done, b + 1)
                    if not (is_first(i) and u == 0):
                        dve.wait_ge(tp_ready, CH * b)
                    for t in range(SUB):
                        v.tensor_scalar(xn[:, t, :], raw[u][:, t, :], mv[:, t, 0:1], rstd[:, t:t + 1],
                                        ALU.subtract, ALU.mult).then_inc(norm_done, 1)

                def low(i, u, c):
                    b = 2 * i + u
                    dve.wait_ge(xt_hi_done, CH * b + c + 1)
                    v.tensor_tensor(xt_lo[u][:, c, :], tp[c % 2][:], xt_hi[u][:, c, :],
                                    ALU.subtract).then_inc(xt_lo_done, 1)

                def rotate(i, u, t):
                    n, r = SUB * (2 * i + u) + t, t % 2
                    dve.wait_ge(k_ready, n + 1)
                    v.tensor_tensor(kf[r], kp[r][:], k.kv_bias[:, 0:D], ALU.add).then_inc(k_biased, 1)
                    dve.wait_ge(k_biased, n + 1)
                    if not (is_first(i) and u == 0 and t < 2):
                        dve.wait_ge(k_added, n - 1)
                    halves = kf[r].rearrange("p (h f) -> p h f", f=HD // 2)
                    heads = kf[r].rearrange("p (h s f) -> p h s f", s=2, f=HD // 2)
                    turned = k_sin[r][:].rearrange("p (h s f) -> p h s f", s=2, f=HD // 2)
                    cos = tab[u][:, t, 0:HD // 2].unsqueeze(1)
                    sin = tab[u][:, t, HD // 2:HD].unsqueeze(1)
                    v.tensor_tensor(k_cos[r][:].rearrange("p (h f) -> p h f", f=HD // 2), halves,
                                    cos.to_broadcast([P, D // (HD // 2), HD // 2]), ALU.mult).then_inc(k_mult, 1)
                    v.scalar_tensor_tensor(out=turned[:, :, 0, :], in0=heads[:, :, 1, :], scalar=-1.0,
                                           in1=sin.to_broadcast([P, D // HD, HD // 2]),
                                           op0=ALU.mult, op1=ALU.mult).then_inc(k_mult, 1)
                    v.tensor_tensor(turned[:, :, 1, :], heads[:, :, 0, :],
                                    sin.to_broadcast([P, D // HD, HD // 2]), ALU.mult).then_inc(k_mult, 1)

                def values(i, u, t):
                    n = SUB * (2 * i + u) + t
                    dve.wait_ge(v_ready, n + 1)
                    if not is_first(i) and t == 0:
                        dve.wait_ge(stored[u], 48 * i)
                    v.tensor_tensor(vo[u][:, :, t, :], vp[:].rearrange("p (a d) -> p a d", a=PAIRS),
                                    k.kv_bias[:, D:2 * D].rearrange("p (a d) -> p a d", a=PAIRS),
                                    ALU.add).then_inc(v_copied, 1)

                def unit_max(b, column, unit):
                    dve.wait_ge(mx_ready, UNITS * b + unit + 1)
                    v.tensor_reduce(k.pmax[:, unit, column], mx[:], AX_X, ALU.max).then_inc(mx_done, 1)

                dve.sem_inc(stats_done, SUB)
                dve.sem_inc(mv_done, SUB)
                dve.sem_inc(var_done, 1)
                dve.sem_inc(norm_done, SUB)
                for c in range(CH):
                    low(0, 0, c)

                def body(i, u):
                    more = not is_last(i, u)
                    nxt = succ(i, u) if more else None
                    b = 2 * i + u
                    column = slice(KB - 1, KB) if is_first(i) and u == 0 else bass.ds(b - 1, 1)
                    if more:
                        norm_stats(*nxt)
                    rotate(i, u, 0)
                    unit_max(b, column, 0)
                    rotate(i, u, 1)
                    unit_max(b, column, 1)
                    if more:
                        normalise(*nxt)
                    values(i, u, 0)
                    unit_max(b, column, 2)
                    rotate(i, u, 2)
                    unit_max(b, column, 3)
                    values(i, u, 1)
                    unit_max(b, column, 4)
                    rotate(i, u, 3)
                    unit_max(b, column, 5)
                    if more:
                        low(*nxt, 0)
                        low(*nxt, 1)
                    values(i, u, 2)
                    unit_max(b, column, 6)
                    if more:
                        low(*nxt, 2)
                        low(*nxt, 3)
                    values(i, u, 3)
                    unit_max(b, column, 7)

                over_blocks(dve, body)
                for unit in range(UNITS):
                    unit_max(CTX_BLOCKS, slice(CTX_BLOCKS - 1, CTX_BLOCKS), unit)

            @block.scalar
            def _(act):
                a = nc.scalar

                def high(i, u, c):
                    b = 2 * i + u
                    act.wait_ge(tp_ready, CH * b + c + 1)
                    if not is_first(i) and c == 0:
                        act.wait_ge(v_ready, SUB * (b - 1))
                    a.activation(xt_hi[u][:, c, :], tp[c % 2][:], ACT.Copy).then_inc(xt_hi_done, 1)

                def key_high(i, u, t):
                    n, r = SUB * (2 * i + u) + t, t % 2
                    act.wait_ge(k_added, n + 1)
                    if not (is_first(i) and u == 0 and t < 2):
                        act.wait_ge(ktp_ready, n - 1)
                    a.activation(kr_hi[r][:], kr[r][:], ACT.Copy).then_inc(k_hi_done, 1)

                def keys_out(i, u, t):
                    n = SUB * (2 * i + u) + t
                    act.wait_ge(ktp_ready, n + 1)
                    if not is_first(i) and t == 0:
                        act.wait_ge(stored[u], 48 * i)
                    if not (is_first(i) and u == 0) and t == 0:
                        act.wait_ge(mx_ready, UNITS * (2 * i + u))
                    a.activation(kt[u].rearrange("p l a n -> p (l a) n")[:, :, t * P:(t + 1) * P],
                                 ktp[t % 2][:].rearrange("p l a n -> p (l a) n"), ACT.Copy).then_inc(kt_copied, 1)

                for c in range(CH):
                    high(0, 0, c)

                def body(i, u):
                    more = not is_last(i, u)
                    nxt = succ(i, u) if more else None
                    key_high(i, u, 0)
                    key_high(i, u, 1)
                    keys_out(i, u, 0)
                    key_high(i, u, 2)
                    keys_out(i, u, 1)
                    if more:
                        high(*nxt, 0)
                        high(*nxt, 1)
                    key_high(i, u, 3)
                    if more:
                        high(*nxt, 2)
                        high(*nxt, 3)
                    keys_out(i, u, 2)
                    keys_out(i, u, 3)

                over_blocks(act, body)

            @block.tensor
            def _(pe):
                t_ = nc.tensor

                def transposes(i, u, c):
                    b = 2 * i + u
                    pe.wait_ge(norm_done, SUB * b + SUB)
                    if not (is_first(i) and u == 0 and c < 2):
                        pe.wait_ge(xt_lo_done, CH * b + c - 1)
                    for t in range(SUB):
                        m = t_.transpose(tp[c % 2][:, t * P:(t + 1) * P], xn[:, t, c * P:(c + 1) * P], k.ident[:])
                    m.then_inc(tp_ready, 1)

                def project(i, u, t, out, off, back, free, ready):
                    b = 2 * i + u
                    n = SUB * b + t
                    pe.wait_ge(xt_lo_done, CH * b + CH)
                    if not (is_first(i) and u == 0 and t < back):
                        pe.wait_ge(free, n - back + 1)
                    rows = slice(t * P, (t + 1) * P)
                    for c in range(CH):
                        m = product3(t_, out[:], (xt_hi[u][:, c, rows], xt_lo[u][:, c, rows]),
                                     (k.wg_hi[:, c, off:off + D], k.wg_lo[:, c, off:off + D]),
                                     c == 0, c == CH - 1)
                    m.then_inc(ready, 1)

                def keys(i, u, t):
                    project(i, u, t, kp[t % 2], 0, 2, k_biased, k_ready)

                def values(i, u, t):
                    project(i, u, t, vp, D, 1, v_copied, v_ready)

                def key_transposes(i, u, t):
                    n = SUB * (2 * i + u) + t
                    pe.wait_ge(k_lo_done, n + 1)
                    if not (is_first(i) and u == 0 and t < 2):
                        pe.wait_ge(kt_copied, n - 1)
                    for hl, part in enumerate((kr_hi, kr_lo)):
                        for p in range(PAIRS):
                            m = t_.transpose(ktp[t % 2][:, hl, p, :], part[t % 2][:, p * P:(p + 1) * P], k.ident16[:])
                    m.then_inc(ktp_ready, 1)

                def max_unit(i, u, unit):
                    b = 2 * i + u
                    if unit == 0 and not (is_first(i) and u == 0):
                        pe.wait_ge(kt_copied, SUB * b)
                    if not (is_first(i) and u == 0 and unit == 0):
                        pe.wait_ge(mx_done, UNITS * b + unit)
                    head, qt = unit // TT, unit % TT
                    part = slice(HD * head, HD * (head + 1))
                    t_.matmul(mx[:], k.q_hi[part, head, qt * P:(qt + 1) * P], kt[1 - u][part, 0, 0, :],
                              start=True, stop=True).then_inc(mx_ready, 1)

                for c in range(CH):
                    transposes(0, 0, c)

                def body(i, u):
                    more = not is_last(i, u)
                    nxt = succ(i, u) if more else None
                    keys(i, u, 0)
                    max_unit(i, u, 0)
                    keys(i, u, 1)
                    max_unit(i, u, 1)
                    values(i, u, 0)
                    max_unit(i, u, 2)
                    keys(i, u, 2)
                    max_unit(i, u, 3)
                    key_transposes(i, u, 0)
                    values(i, u, 1)
                    max_unit(i, u, 4)
                    keys(i, u, 3)
                    max_unit(i, u, 5)
                    key_transposes(i, u, 1)
                    if more:
                        transposes(*nxt, 0)
                        transposes(*nxt, 1)
                    values(i, u, 2)
                    max_unit(i, u, 6)
                    if more:
                        transposes(*nxt, 2)
                        transposes(*nxt, 3)
                    values(i, u, 3)
                    max_unit(i, u, 7)
                    key_transposes(i, u, 2)
                    key_transposes(i, u, 3)

                over_blocks(pe, body)
                for unit in range(UNITS):
                    max_unit(PAIRS_OF_BLOCKS, 0, unit)


def attention_phase(k):
    nc = k.nc
    STEPS = KB * SUB
    P_BUFS = 4
    with ExitStack() as ctx:
        def sb(name, shape, dt):
            return ctx.enter_context(nc.sbuf_tensor(name, shape, dt))

        def sem(name):
            return ctx.enter_context(nc.semaphore(name))

        def pb(name, shape, dt):
            return ctx.enter_context(nc.psum_tensor(name, shape, dt))

        ka = [sb(f"ka{n}", [P, 2, BLK], F16) for n in range(2)]
        kh = [sb(f"kh{n}", [HD + 1, 2, BLK], F16) for n in range(2)]
        vb = [sb(f"vb{n}", [P, SUB, P], F32) for n in range(2)]
        km = [sb(f"km{n}", [HD, 2, BLK], F16) for n in range(2)]
        probs = [sb(f"probs{n}", [P, 2 * TOK], F32) for n in range(P_BUFS)]
        sum_dve = rows(k.h_lo, 8, 4)
        sum_pool = sb("sum_pool", [P, 2 * TOK], F32)
        pmax = k.pmax
        rmax = sb("rmax", [P, UNITS], F32)
        rneg = sb("rneg", [P, UNITS], F32)
        zero = sb("zero", [P, P], F16)
        o_sum, o_raw = ([k.res[:, 2 * m + n] for n in range(2)] for m in range(2))
        o_inv, o_t = rows(k.h_lo, 12, 2), rows(k.h_lo, 14, 2)
        sc = [pb(f"sc{n}", [P, 2 * TOK], F32) for n in range(2)]
        mx = [pb(f"mx{n}", [P, BLK], F32) for n in range(2)]
        pv = pb("pv", [P, TOK], F32)
        side = pb("side", [P, TOK], F32)

        loaded = [sem(f"a_loaded{n}") for n in range(2)]
        m_loaded = [sem(f"m_loaded{n}") for n in range(2)]
        consts = sem("a_consts")
        scores_ready, exp_done, pv_done = (sem(n) for n in ("scores_ready", "exp_done", "pv_done"))
        mx_ready, mx_done, rmax_done, rneg_done, rows_ready, rows_done = (sem(n) for n in (
            "mx_ready", "mx_done", "rmax_done", "rneg_done", "rows_ready", "rows_done"))
        dve_cleared, pool_cleared, dve_summed, pool_summed, sums_ready, out_copied, out_inv, out_scaled = (
            sem(n) for n in ("dve_cleared", "pool_cleared", "dve_summed", "pool_summed", "sums_ready",
                             "out_copied", "out_inv", "out_scaled"))
        passed = sem("a_passed")
        oh_done, ol_done = sem("oh_done"), sem("ol_done")
        w_staged, w_hi, w_lo = sem("a_w_staged"), sem("a_w_hi"), sem("a_w_lo")
        hi_pieces, lo_pieces, staged_pieces = (w[:].rearrange("p a c n -> p (a c) n") for w in (k.wt_hi, k.wt_lo, k.stage))

        with nc.Block() as block:
            @block.sync
            def _(sp):
                def load(g, n):
                    for hl in range(2):
                        rows = k.keys[hl, g].rearrange("(s r) n -> r s n", s=2)
                        sp.dma_start(ka[n][hl * HD:(hl + 1) * HD], rows).then_inc(loaded[n], 16)
                    sp.dma_start(kh[n][0:HD], k.keys[0, g].rearrange("(s r) n -> r s n", s=2)).then_inc(loaded[n], 16)
                    sp.dma_start(vb[n][:], k.values[g]).then_inc(loaded[n], 16)

                def load_m(g, n):
                    sp.dma_start(km[n][:], k.keys[0, g].rearrange("(s r) n -> r s n", s=2)).then_inc(m_loaded[n], 16)

                def load_weights(p):
                    if p > 1:
                        sp.wait_ge(w_lo, PIECES * (p - 1))
                    for n in range(STAGES):
                        c = STAGES * (p - 1) + n
                        w = ((k.xwo, k.wk[0], k.wq_l[0], k.wv[0], k.wo[0])[c] if c < 5
                             else k.wf1[0, :, (c - 5) * D:(c - 4) * D])
                        sp.dma_start(k.stage[:, n], w.rearrange("(c p) n -> p c n", p=P)).then_inc(w_staged, 16)

                def next_m(g, n):
                    sp.wait_ge(mx_ready, UNITS * (g + 1 - KB))
                    sp.sem_inc(passed, 1)
                    load_m(g + 2, n)

                def next_s(g, n):
                    sp.wait_ge(pv_done, P_BUFS + SUB * (g + 1))
                    sp.sem_inc(passed, 1)
                    load(g + 2, n)

                for g in (KB, KB + 1):
                    load_m(g, g % 2)
                load(0, 0)
                load(1, 1)
                load_weights(1)
                both = BLOCKS - KB - 2
                assert KB % 2 and both == 3 * KB - 2 and PAIRS == 4
                with sp.Fori(0, KB) as i:
                    for u in range(2):
                        next_s(2 * i + u, u)
                        next_m(2 * i + u + KB, (u + KB) % 2)
                load_weights(2)
                with sp.Fori(KB, both // 2) as i:
                    for u in range(2):
                        next_s(2 * i + u, u)
                        next_m(2 * i + u + KB, (u + KB) % 2)
                next_s(both - 1, (both - 1) % 2)
                next_m(both - 1 + KB, (both - 1 + KB) % 2)
                for g in range(both, 3 * KB):
                    next_s(g, g % 2)
                load_weights(3)
                with sp.Fori(0, (KB - 3) // 2) as i:
                    for u in range(2):
                        next_s(3 * KB + 2 * i + u, (3 * KB + u) % 2)
                next_s(BLOCKS - 3, (BLOCKS - 3) % 2)

            @block.gpsimd
            def _(pool):
                g = nc.gpsimd
                g.memset(zero[:], 0.0).then_inc(consts, 1)
                pool.sem_inc(pool_summed, 2)
                for p in range(PAIRS):
                    if p:
                        pool.wait_ge(sums_ready, p)
                    g.memset(sum_pool[:], 0.0).then_inc(pool_cleared, 1)
                    pool.wait_ge(pool_cleared, p + 1)

                    def odd_sums(b):
                        for j in (1, 3):
                            step = p * STEPS + SUB * b + j
                            odd = p * (STEPS // 2) + 2 * b + j // 2
                            pool.wait_ge(exp_done, 2 + step + 1)
                            pool.wait_ge(pool_summed, 2 + odd)
                            g.tensor_tensor(sum_pool[:], sum_pool[:], probs[j][:], ALU.add).then_inc(pool_summed, 1)

                    with pool.Fori(0, KB - PIECES if p else KB) as b:
                        odd_sums(b)
                    if p:
                        pool.wait_ge(w_staged, 16 * STAGES * p)
                        with pool.Fori(KB - PIECES, KB) as b:
                            odd_sums(b)
                            n = b - (KB - PIECES)
                            pool.wait_ge(w_hi, PIECES * (p - 1) + n + 1)
                            pool.sem_inc(passed, 1)
                            at = bass.ds(4 * XWO + PIECES * (p - 1) + n, 1)
                            g.tensor_tensor(lo_pieces[:, at, :], staged_pieces[:, bass.ds(n, 1), :],
                                            hi_pieces[:, at, :], ALU.subtract).then_inc(w_lo, 1)

            @block.vector
            def _(dve):
                v = nc.vector

                def unit_max(p, b, j, w):
                    unit = 2 * j + w
                    dve.wait_ge(mx_ready, UNITS * ((p - 1) * KB + b) + unit + 1)
                    v.tensor_reduce(pmax[:, unit, bass.ds(b, 1)], mx[w][:], AX_X, ALU.max).then_inc(mx_done, 1)

                def pair_max(p):
                    if p:
                        dve.wait_ge(mx_done, 2 + UNITS * KB * p)
                    v.tensor_reduce(rmax[:], pmax[:], AX_X, ALU.max).then_inc(rmax_done, 1)
                    dve.wait_ge(rmax_done, p + 1)
                    if p:
                        dve.wait_ge(rows_ready, p)
                    v.tensor_scalar(rneg[:], rmax[:], -1.0 / M_UNIT, None, ALU.mult).then_inc(rneg_done, 1)

                def out_scale(p):
                    dve.wait_ge(out_copied, 2 * (p + 1))
                    v.reciprocal(o_inv, o_sum[p % 2]).then_inc(out_inv, 1)
                    dve.wait_ge(out_inv, p + 1)
                    v.tensor_tensor(o_t, o_raw[p % 2], o_inv, ALU.mult).then_inc(out_scaled, 1)

                def out_low(p):
                    dve.wait_ge(oh_done, p + 1)
                    v.tensor_tensor(k.o_lo[:, p, :], o_t, k.o_hi[:, p, :], ALU.subtract).then_inc(ol_done, 1)

                for n in range(2):
                    v.memset(kh[n][HD:HD + 1], M_UNIT).then_inc(consts, 1)
                dve.sem_inc(mx_done, 2)
                dve.sem_inc(dve_summed, 2)
                pair_max(0)
                for p in range(PAIRS):
                    if p:
                        dve.wait_ge(sums_ready, p)
                    v.memset(sum_dve, 0.0).then_inc(dve_cleared, 1)
                    dve.wait_ge(dve_cleared, p + 1)
                    with dve.Fori(0, KB) as b:
                        for j in range(SUB):
                            if p + 1 < PAIRS:
                                for w in range(2):
                                    unit_max(p + 1, b, j, w)
                            if j % 2 == 0:
                                step = p * STEPS + SUB * b + j
                                even = p * (STEPS // 2) + 2 * b + j // 2
                                dve.wait_ge(exp_done, 2 + step + 1)
                                dve.wait_ge(dve_summed, 2 + even)
                                v.tensor_tensor(sum_dve, sum_dve, probs[j][:], ALU.add).then_inc(dve_summed, 1)
                    if p + 1 < PAIRS:
                        pair_max(p + 1)
                    if p >= 2:
                        out_low(p - 2)
                    if p:
                        out_scale(p - 1)
                out_low(PAIRS - 2)
                out_scale(PAIRS - 1)
                out_low(PAIRS - 1)

            @block.scalar
            def _(act):
                a = nc.scalar
                act.sem_inc(exp_done, 2)

                def row_maxima(p):
                    act.wait_ge(rows_ready, p + 1)
                    for s in range(2):
                        a.activation(k.q_lo[HD:HD + 1, 2 * p + s, :], side[HD * s:HD * s + 1, :],
                                     ACT.Copy).then_inc(rows_done, 1)

                def out_high(p):
                    act.wait_ge(out_scaled, p + 1)
                    a.activation(k.o_hi[:, p, :], o_t, ACT.Copy).then_inc(oh_done, 1)

                row_maxima(0)
                for p in range(PAIRS):

                    def exponentials(b):
                        for j in range(SUB):
                            step = p * STEPS + SUB * b + j
                            act.wait_ge(scores_ready, step + 1)
                            act.wait_ge(pv_done, step + 1)
                            act.wait_ge(dve_summed if j % 2 == 0 else pool_summed,
                                        p * (STEPS // 2) + 2 * b + j // 2 + 1)
                            a.activation(probs[j][:], sc[j % 2][:], ACT.Exp).then_inc(exp_done, 1)

                    with act.Fori(0, KB - PIECES if p else KB) as b:
                        exponentials(b)
                    if p:
                        act.wait_ge(w_staged, 16 * STAGES * p)
                        with act.Fori(KB - PIECES, KB) as b:
                            exponentials(b)
                            n = b - (KB - PIECES)
                            a.activation(hi_pieces[:, bass.ds(4 * XWO + PIECES * (p - 1) + n, 1), :],
                                         staged_pieces[:, bass.ds(n, 1), :], ACT.Copy).then_inc(w_hi, 1)
                    if p + 1 < PAIRS:
                        row_maxima(p + 1)
                    act.wait_ge(sums_ready, p + 1)
                    if p >= 2:
                        act.wait_ge(out_scaled, p - 1)
                    a.activation(o_sum[p % 2], side[:], ACT.Copy).then_inc(out_copied, 1)
                    a.activation(o_raw[p % 2], pv[:], ACT.Copy).then_inc(out_copied, 1)
                    if p:
                        out_high(p - 1)
                out_high(PAIRS - 1)

            @block.tensor
            def _(pe):
                t_ = nc.tensor

                def max_unit(p, i, u, j, w):
                    b, slot, unit = 2 * i + u, (p * KB + u) % 2, 2 * j + w
                    if unit == 0:
                        before = (KB + 1 - slot) // 2
                        pe.wait_ge(m_loaded[slot], 16 * ((p * KB + u) // 2 + i + 1 - before))
                    pe.wait_ge(mx_done, UNITS * ((p - 1) * KB + b) + unit + 1)
                    head, qt = unit // TT, unit % TT
                    t_.matmul(mx[w][:], k.q_hi[0:HD, 2 * p + head, qt * P:(qt + 1) * P],
                              km[slot][:, head, :], start=True, stop=True).then_inc(mx_ready, 1)

                def scores(p, i, u, j):
                    step, slot = p * STEPS + SUB * (2 * i + u) + j, (p * KB + u) % 2
                    if j == 0:
                        pe.wait_ge(loaded[slot], 64 * ((p * KB + u) // 2 + i + 1))
                    pe.wait_ge(exp_done, step + 1)
                    for s in range(2):
                        out, cols = sc[j % 2][:, s * TOK:(s + 1) * TOK], slice(j * P, (j + 1) * P)
                        t_.matmul(out, ka[slot][:, s, cols], k.q_hi[:, 2 * p + s, :], start=True, stop=False)
                        m = t_.matmul(out, kh[slot][:, s, cols], k.q_lo[:, 2 * p + s, :], start=False, stop=True)
                    m.then_inc(scores_ready, 1)

                def weigh(p, i, u, j, last):
                    step, slot = p * STEPS + SUB * (2 * i + u) + j, (p * KB + u) % 2
                    pe.wait_ge(exp_done, 2 + step + 1)
                    for s in range(2):
                        rows = slice(s * HD, (s + 1) * HD)
                        m = t_.matmul(pv[rows, :], vb[slot][:, j, rows], probs[j][:, s * TOK:(s + 1) * TOK],
                                      start=False, stop=last)
                    m.then_inc(pv_done, 1)

                def rows_of_maxima(p):
                    pe.wait_ge(rneg_done, p + 1)
                    if p >= 2:
                        pe.wait_ge(out_copied, 2 * (p - 1))
                    for s in range(2):
                        for q in range(TT):
                            unit = s * TT + q
                            m = t_.matmul(side[s * HD:s * HD + 1, q * P:(q + 1) * P], rneg[:, unit:unit + 1],
                                          k.ident[:], start=True, stop=True)
                    m.then_inc(rows_ready, 1)

                def row_sums(p):
                    pe.wait_ge(dve_summed, 2 + (p + 1) * (STEPS // 2))
                    pe.wait_ge(pool_summed, 2 + (p + 1) * (STEPS // 2))
                    pe.wait_ge(rows_done, 2 * min(p + 2, PAIRS))
                    for s in range(2):
                        for n, part in enumerate((sum_dve, sum_pool)):
                            m = t_.matmul(side[s * HD:(s + 1) * HD, :], k.ones[:, 0:HD],
                                          part[:, s * TOK:(s + 1) * TOK], start=n == 0, stop=n == 1)
                    m.then_inc(sums_ready, 1)

                def block_steps(p, i, u, last):
                    for j in range(SUB):
                        if j + 1 < SUB:
                            scores(p, i, u, j + 1)
                        elif not last:
                            scores(p, i, u + 1, 0) if u == 0 else scores(p, i + 1, 0, 0)
                        if p + 1 < PAIRS:
                            for w in range(2):
                                max_unit(p + 1, i, u, j, w)
                        weigh(p, i, u, j, last and j == SUB - 1)

                pe.sem_inc(pv_done, P_BUFS)
                rows_of_maxima(0)
                pe.wait_ge(consts, 3)
                for p in range(PAIRS):
                    pe.wait_ge(rows_done, 2 * (p + 1))
                    scores(p, 0, 0, 0)
                    if p:
                        row_sums(p - 1)
                        pe.wait_ge(out_copied, 2 * p)
                    t_.matmul(pv[:], zero[:], k.q_hi[:, 0, :], start=True, stop=False)
                    with pe.Fori(0, (KB - 1) // 2) as i:
                        for u in range(2):
                            block_steps(p, i, u, False)
                    block_steps(p, (KB - 1) // 2, 0, True)
                    if p + 1 < PAIRS:
                        rows_of_maxima(p + 1)
                row_sums(PAIRS - 1)


LAYERS = 8
FF = 2048
FT = FF // P
EPS_LAYER = 1e-6
EPS_Z = 1e-6
HALF = TOK // 2
NQ = FF // D
K_, Q_, V_ = 0, 1, 2
GROUP_ORDER = ([(K_, at, half) for half in range(2) for at in range(4)]
               + [(w, at, half) for w in (Q_, V_) for at in range(4) for half in range(2)])
SECOND = 4
LAST_TILE = 2
NEG, PLUS, BV, BF1, COLS = 0, 8, 16, 20, 36


def layers_phase(k):
    nc = k.nc
    with ExitStack() as ctx:
        def sb(name, shape, dt):
            return ctx.enter_context(nc.sbuf_tensor(name, shape, dt))

        def sem(name):
            return ctx.enter_context(nc.semaphore(name))

        def pb(name, shape, dt):
            return ctx.enter_context(nc.psum_tensor(name, shape, dt))

        wt_hi, wt_lo = k.wt_hi, k.wt_lo
        stage = [k.stage[:, n] for n in range(STAGES)]
        xt_hi = sb("l_xt_hi", [P, CH, TOK], F16)
        xt_lo = sb("l_xt_lo", [P, CH, TOK], BF16)
        h_hi = sb("h_hi", [P, FT, TOK], F16)
        h_lo = k.h_lo
        hf = [sb(f"hf{n}", [P, 4, HALF], F32) for n in range(2)]
        key_t = h_hi[:, 0:8, :].rearrange("p a n -> p (a n)").bitcast(F32).rearrange("p (a n) -> p a n", a=CH)
        qry_t = h_hi[:, 8:16, :].rearrange("p a n -> p (a n)").bitcast(F32).rearrange("p (a n) -> p a n", a=CH)
        val_hi = h_lo[:, 0:4, :].bitcast(F16)
        val_lo = h_lo[:, 4:8, :]
        den = [hf[n][:, 0:2, :].rearrange("p a n -> p (a n)") for n in range(2)]
        inv = [hf[n][:, 2:4, :].rearrange("p a n -> p (a n)") for n in range(2)]
        kv_prod = [h_lo[:, n:n + 1, :].rearrange("p a n -> p (a n)").bitcast(F32) for n in (12, 15)]
        relu_t = [h_lo[:, 13 + n:14 + n, :].rearrange("p a n -> p (a n)").bitcast(F32) for n in range(2)]
        exp_t = [sb(f"exp_t{n}", [P, HALF], F32) for n in range(2)]
        res = k.res
        pre = [sb(f"pre{n}", [P, D], F32) for n in range(2)]
        bc_attn = sb("bc_attn", [P, 3, D], F32)
        bc_ff = sb("bc_ff", [P, 3, D], F32)
        vec_rows = sb("vec_rows", [P, 2, P], F32)
        cols = sb("cols", [P, LAYERS, COLS], F32)
        cur = sb("cur", [P, COLS], F32)
        stats = sb("l_stats", [P, TT, 6], F32)
        mv = sb("l_mv", [P, TT, 2], F32)
        var_eps = sb("l_var_eps", [P, TT], F32)
        rstd = sb("l_rstd", [P, TT], F32)
        ks_part = sb("ks_part", [P, CH, 2], F32)
        kv_part = sb("kv_part", [P, CH, 2], F32)
        ks = sb("ks", [P, CH], F32)
        kv = sb("kv", [P, CH], F32)
        mm = [pb(f"l_mm{n}", [P, D], F32) for n in range(4)]
        tok = [pb(f"l_tok{n}", [P, D], F32) for n in range(2)]
        tp = [pb(f"l_tp{n}", [P, CH, P], F32) for n in range(2)]

        def half_of(b):
            return b[:, 0:2, :].rearrange("p a n -> p (a n)") if b in tp else b[:, 0:HALF]

        def bank(g):
            return mm[g] if g < 4 else [tok[0], tok[1], tp[0]][g - 4] if g < 7 else mm[(g - 7) % 4]

        def bank_freed(g):
            return g - 6 if g < 11 else g - 3

        attn_out = [tp[n][:].rearrange("p c n -> p (c n)") for n in range(2)] + [t[:] for t in tok]

        staged = [sem(f"staged{n}") for n in range(STAGES)]
        vec_in, zeroed, cols_ready, cols_done, cur_done = (sem(n) for n in (
            "l_vec_in", "l_zeroed", "cols_ready", "cols_done", "cur_done"))
        bc_attn_in, bc_ff_in = sem("bc_attn_in"), sem("bc_ff_in")
        w_hi, w_lo_dve, w_lo_pool = sem("w_hi"), sem("w_lo_dve"), sem("w_lo_pool")
        proj_ready, relu_done, exp_done, exp_rounded, proj_used = (sem(n) for n in (
            "proj_ready", "relu_done", "l_exp_done", "exp_rounded", "proj_used"))
        ks_done, den_done, inv_done, qz_done, kv_done, val_hi_done, val_lo_done = (sem(n) for n in (
            "ks_done", "den_done", "inv_done", "qz_done", "kv_done", "val_hi_done", "val_lo_done"))
        tok_ready, tok_biased, tok_gelu, tok_added = (sem(n) for n in (
            "tok_ready", "tok_biased", "tok_gelu", "tok_added"))
        stats_done, mv_done, var_done, rstd_done, scaled, normed = (sem(n) for n in (
            "l_stats_done", "l_mv_done", "l_var_done", "l_rstd_done", "l_scaled", "normed"))
        tp_ready, xt_hi_done, xt_lo_done = (sem(n) for n in ("l_tp_ready", "l_xt_hi_done", "l_xt_lo_done"))
        f1_ready, f1_gelu, h_hi_done, h_lo_done = (sem(n) for n in ("f1_ready", "f1_gelu", "h_hi_done", "h_lo_done"))
        final_added, projected, stream_added = sem("final_added"), sem("projected"), sem("stream_added")
        ahead = sem("l_ahead")
        passed = sem("l_passed")

        def is_last(l):
            return isinstance(l, int)

        def over_layers(eng, body):
            with eng.Fori(0, LAYERS - 1) as l:
                body(l)
            body(LAYERS - 1)

        def stage_of(c):
            return c % STAGES

        def source(l, c):
            if c < KQVO:
                w = k.wf2[l, c * D:(c + 1) * D, :]
            elif is_last(l):
                w = k.ef1[:, (c - KQVO) * D:(c - KQVO + 1) * D]
            elif c < F1:
                w = (k.wk, k.wq_l, k.wv, k.wo)[c - KQVO][l + 1]
            else:
                w = k.wf1[l + 1, :, (c - F1) * D:(c - F1 + 1) * D]
            return w.rearrange("(c p) n -> p c n", p=P)

        nc.clear_and_free_semaphores(k.spare_semaphores)
        with nc.Block() as block:
            @block.sync
            def _(sp):
                for n, (b, rows) in enumerate(((k.bk, 0), (k.bq, 32), (k.bv, 64))):
                    sp.dma_start(vec_rows[rows:rows + 32, 0, :],
                                 b.rearrange("l (c p) -> (l c) p", p=P)).then_inc(vec_in, 16)
                sp.dma_start(vec_rows[:, 1, :], k.bf1.rearrange("l (c p) -> (l c) p", p=P)).then_inc(vec_in, 16)
                def broadcast(dst, vecs, l, done):
                    for n, b in enumerate(vecs):
                        sp.dma_start(dst[:, n, :], b[l].unsqueeze(0).to_broadcast([P, D])).then_inc(done, 16)

                def body(l):
                    for c in range(CHUNKS):
                        if c < STAGES:
                            sp.wait_ge(w_lo_dve, 32 * l + 4 * (c + 9 - STAGES))
                        elif c < 4 + STAGES:
                            sp.wait_ge(w_lo_pool, 16 * l + 4 * (c - STAGES + 1))
                        else:
                            sp.wait_ge(w_lo_dve, 32 + 32 * l + 4 * (c - STAGES - 3))
                        sp.sem_inc(passed, 1)
                        st = stage_of(c)
                        sp.dma_start(stage[st], source(l, c)).then_inc(staged[st], 16)
                        if c == 2:
                            sp.wait_ge(normed, TT + 2 * TT * l)
                            sp.sem_inc(passed, 1)
                            broadcast(bc_attn, (k.bo, k.ln1_s, k.ln1_b), l, bc_attn_in)
                            broadcast(bc_ff, (k.bf2, k.ln2_s, k.ln2_b), l, bc_ff_in)

                over_layers(sp, body)
                for m in range(2):
                    sp.wait_ge(w_lo_dve, 32 * LAYERS + 4 * (9 + m - 3))
                    rows = k.ef2[m * D:(m + 1) * D, :].rearrange("(c p) n -> p c n", p=P)
                    sp.dma_start(stage[m], rows).then_inc(ahead, 16)
                sp.wait_ge(ahead, 32)

            @block.gpsimd
            def _(pool):
                g = nc.gpsimd
                g.memset(vec_rows[96:128, 0, :], 0.0).then_inc(zeroed, 1)
                pool.wait_ge(zeroed, 1)

                def inverse_std(n, t):
                    pool.wait_ge(var_done, n + 1)
                    g.tensor_tensor(rstd[:, t:t + 1], var_eps[:, t:t + 1], k.neg_half[:, 0:1],
                                    ALU.pow).then_inc(rstd_done, 1)

                for t in range(TT):
                    inverse_std(t, t)

                def body(l):
                    pool.wait_ge(proj_ready, 24 * l + 1)
                    def f2_low(c):
                        for n in range(4):
                            pool.wait_ge(w_hi, 32 + 48 * l + 4 * c + n + 1)
                            g.tensor_tensor(wt_lo[:, c, n, :], stage[stage_of(c)][:, n, :], wt_hi[:, c, n, :],
                                            ALU.subtract).then_inc(w_lo_pool, 1)

                    def weighted(at):
                        pool.wait_ge(inv_done, 4 * l + at + 1)
                        g.tensor_tensor(qry_t[:, at, :], qry_t[:, at, :], inv[at % 2], ALU.mult).then_inc(qz_done, 1)

                    f2_low(0)
                    f2_low(1)
                    weighted(0)
                    weighted(1)
                    weighted(2)
                    f2_low(2)
                    weighted(3)
                    f2_low(3)
                    for t in range(2 * TT):
                        inverse_std(TT + 2 * TT * l + t, t % TT)

                over_layers(pool, body)

            @block.vector
            def _(dve):
                v = nc.vector

                def weight_low(done, slot, st, n):
                    dve.wait_ge(w_hi, done)
                    v.tensor_tensor(wt_lo[:, slot, n, :], stage[st][:, n, :], wt_hi[:, slot, n, :],
                                    ALU.subtract).then_inc(w_lo_dve, 1)

                def low(m, t):
                    dve.wait_ge(xt_hi_done, m + 1)
                    v.tensor_tensor(xt_lo[:, :, t * P:(t + 1) * P], tp[t % 2][:], xt_hi[:, :, t * P:(t + 1) * P],
                                    ALU.subtract).then_inc(xt_lo_done, 1)

                def tile_stats(m, t, src, eps):
                    v.bn_stats(stats[:, t, :], src).then_inc(stats_done, 1)
                    dve.wait_ge(stats_done, m + 1)
                    dve.sem_inc(passed, 1)
                    v.bn_aggr(mv[:, t, :], stats[:, t, :]).then_inc(mv_done, 1)
                    dve.wait_ge(mv_done, m + 1)
                    v.tensor_scalar(var_eps[:, t:t + 1], mv[:, t, 1:2], eps, None, ALU.add).then_inc(var_done, 1)

                def tile_bias(l, t, bank, bc):
                    dve.wait_ge(tok_ready, 2 * TT * l + t + 1)
                    v.tensor_tensor(pre[t % 2][:], bank, bc[:, 0, :], ALU.add).then_inc(tok_biased, 1)

                def tile_residual(l, t):
                    n, m, r = 2 * TT * l + t, TT + 2 * TT * l + t, t % TT
                    dve.wait_ge(tok_gelu, n + 1)
                    v.tensor_tensor(res[:, r, :], res[:, r, :], pre[t % 2][:], ALU.add).then_inc(tok_added, 1)
                    dve.wait_ge(tok_added, n + 1)
                    tile_stats(m, r, res[:, r, :], EPS_LAYER)

                def tile_norm(l, t, bc):
                    n, m, r = 2 * TT * l + t, TT + 2 * TT * l + t, t % TT
                    v.scalar_tensor_tensor(out=res[:, r, :], in0=res[:, r, :], scalar=mv[:, r, 0:1],
                                           in1=bc[:, 1, :], op0=ALU.subtract, op1=ALU.mult).then_inc(scaled, 1)
                    dve.wait_ge(scaled, n + 1)
                    dve.wait_ge(rstd_done, m + 1)
                    v.scalar_tensor_tensor(out=res[:, r, :], in0=res[:, r, :], scalar=rstd[:, r:r + 1],
                                           in1=bc[:, 2, :], op0=ALU.mult, op1=ALU.add).then_inc(normed, 1)

                def stream_stats(t):
                    dve.wait_ge(projected, t + 1)
                    v.tensor_tensor(k.x_sb[:, t, :], k.x_sb[:, t, :], mm[t][:], ALU.add).then_inc(stream_added, 1)
                    dve.wait_ge(stream_added, t + 1)
                    tile_stats(t, t, k.x_sb[:, t, :], EPS_OUTER)

                def stream_norm(t):
                    dve.wait_ge(rstd_done, t + 1)
                    v.tensor_scalar(res[:, t, :], k.x_sb[:, t, :], mv[:, t, 0:1], rstd[:, t:t + 1],
                                    ALU.subtract, ALU.mult).then_inc(normed, 1)

                stream_stats(0)
                stream_stats(1)
                stream_norm(0)
                stream_stats(2)
                stream_norm(1)
                stream_stats(3)
                stream_norm(2)
                dve.wait_ge(cols_ready, 1)
                kq = tp[0][:, 0, 0:64].rearrange("p (a l c) -> p l a c", a=2, l=LAYERS)
                bv = tp[0][:, 0, 64:96].rearrange("p (l c) -> p l c", l=LAYERS)
                two = cols[:, :, NEG:NEG + 8].rearrange("p l (a c) -> p l a c", a=2)
                plus = cols[:, :, PLUS:PLUS + 8].rearrange("p l (a c) -> p l a c", a=2)
                v.tensor_scalar(two, kq, -1.0, None, ALU.mult).then_inc(cols_done, 1)
                v.tensor_scalar(plus, kq, 1.0, None, ALU.add).then_inc(cols_done, 1)
                v.tensor_copy(cols[:, :, BV:BV + 4], bv).then_inc(cols_done, 1)
                v.tensor_copy(cols[:, :, BF1:BF1 + FT],
                              tp[1][:, 0, :].rearrange("p (l c) -> p l c", l=LAYERS)).then_inc(cols_done, 1)
                stream_norm(3)
                for t in range(TT - 1):
                    low(t, t)
                dve.sem_inc(w_lo_dve, 32)
                dve.wait_ge(cols_done, 4)
                dve.sem_inc(tok_biased, 2)
                v.tensor_copy(cur[:], cols[:, 0, :]).then_inc(cur_done, 1)

                def body(l):
                    last = is_last(l)
                    m0 = TT + 2 * TT * l
                    dve.wait_ge(cur_done, l + 1)

                    def elu1(g, dst, **kw):
                        which, at, half = GROUP_ORDER[g]
                        dve.wait_ge(exp_done, 16 * l + g + 1)
                        v.tensor_scalar(exp_t[g % 2][:], exp_t[g % 2][:], -1.0, 1.0, ALU.add, ALU.add).then_inc(exp_rounded, 1)
                        dve.wait_ge(exp_rounded, 16 * l + g + 1)
                        v.scalar_tensor_tensor(out=dst[:, at, half * HALF:(half + 1) * HALF],
                                               in0=half_of(bank(g)),
                                               scalar=cur[:, PLUS + 4 * which + at:PLUS + 4 * which + at + 1],
                                               in1=exp_t[g % 2][:], op0=ALU.add, op1=ALU.max, **kw).then_inc(proj_used, 1)

                    def inverse(at):
                        dve.wait_ge(proj_used, 24 * l + 8 + 2 * at + 2)
                        v.tensor_scalar(den[at % 2], qry_t[:, at, :], ks[:, at:at + 1], EPS_Z,
                                        ALU.mult, ALU.add).then_inc(den_done, 1)
                        dve.wait_ge(den_done, 4 * l + at + 1)
                        if at >= 2:
                            dve.wait_ge(qz_done, 4 * l + at - 1)
                        v.reciprocal(inv[at % 2], den[at % 2]).then_inc(inv_done, 1)

                    def value_sum(at):
                        for half in range(2):
                            g = 16 + 2 * at + half
                            dve.wait_ge(proj_ready, 24 * l + g + 1)
                            v.scalar_tensor_tensor(out=kv_prod[half], in0=half_of(bank(g)),
                                                   scalar=cur[:, BV + at:BV + at + 1],
                                                   in1=key_t[:, at, half * HALF:(half + 1) * HALF],
                                                   op0=ALU.add, op1=ALU.mult,
                                                   accum_out=kv_part[:, at, half:half + 1]).then_inc(proj_used, 1)
                        dve.wait_ge(proj_used, 24 * l + 16 + 2 * at + 2)
                        v.tensor_tensor(kv[:, at:at + 1], kv_part[:, at, 0:1], kv_part[:, at, 1:2],
                                        ALU.add).then_inc(kv_done, 1)

                    def value_low(at):
                        dve.wait_ge(val_hi_done, 4 * l + at + 1)
                        v.scalar_tensor_tensor(out=val_lo[:, at, :], in0=qry_t[:, at, :], scalar=kv[:, at:at + 1],
                                               in1=val_hi[:, at, :], op0=ALU.mult, op1=ALU.subtract).then_inc(val_lo_done, 1)

                    for g in range(8):
                        if g == LAST_TILE:
                            low(m0 - 1, TT - 1)
                        which, at, half = GROUP_ORDER[g]
                        elu1(g, key_t, accum_out=ks_part[:, at, half:half + 1])
                    dve.wait_ge(proj_used, 24 * l + 8)
                    v.tensor_tensor(ks[:], ks_part[:, :, 0], ks_part[:, :, 1], ALU.add).then_inc(ks_done, 1)
                    elu1(8, qry_t)
                    elu1(9, qry_t)
                    dve.wait_ge(ks_done, l + 1)
                    inverse(0)
                    elu1(10, qry_t)
                    elu1(11, qry_t)
                    inverse(1)
                    elu1(12, qry_t)
                    elu1(13, qry_t)
                    inverse(2)
                    elu1(14, qry_t)
                    elu1(15, qry_t)
                    value_sum(0)
                    inverse(3)
                    value_sum(1)
                    value_low(0)
                    value_sum(2)
                    value_low(1)
                    value_sum(3)
                    value_low(2)
                    value_low(3)
                    dve.wait_ge(bc_attn_in, 48 * l + 48)
                    tile_bias(l, 0, attn_out[0], bc_attn)
                    tile_residual(l, 0)
                    tile_bias(l, 1, attn_out[1], bc_attn)
                    tile_norm(l, 0, bc_attn)
                    tile_residual(l, 1)
                    tile_norm(l, 1, bc_attn)
                    low(m0 + 0, 0)
                    low(m0 + 1, 1)
                    tile_bias(l, 2, attn_out[2], bc_attn)
                    tile_bias(l, 3, attn_out[3], bc_attn)
                    tile_residual(l, 2)
                    tile_residual(l, 3)
                    tile_norm(l, 2, bc_attn)
                    tile_norm(l, 3, bc_attn)
                    low(m0 + 2, 2)
                    low(m0 + 3, 3)
                    for quarter in range(8):
                        half, q = quarter // 4, quarter % 4
                        dve.wait_ge(h_hi_done, 8 * l + quarter + 1)
                        v.tensor_tensor(h_lo[:, 4 * q:4 * q + 4, half * HALF:(half + 1) * HALF], hf[quarter % 2][:],
                                        h_hi[:, 4 * q:4 * q + 4, half * HALF:(half + 1) * HALF],
                                        ALU.subtract).then_inc(h_lo_done, 1)
                        for n in range(2):
                            piece = 2 * quarter + n
                            weight_low(32 + 48 * l + 16 + piece + 1, KQVO + piece // 4, stage_of(KQVO + piece // 4), piece % 4)
                    dve.wait_ge(bc_ff_in, 48 * l + 48)
                    for t in range(TT):
                        for n in range(4):
                            weight_low(32 + 48 * l + 32 + 4 * t + n + 1, F1 + t, stage_of(F1 + t), n)
                        tile_bias(l, TT + t, tok[t % 2][:], bc_ff)
                        tile_residual(l, TT + t)
                        tile_norm(l, TT + t, bc_ff)
                        if t == 1 and not last:
                            dve.wait_ge(f1_gelu, 4 + 32 * l + 32)
                            dve.sem_inc(passed, 1)
                            v.tensor_copy(cur[:], cols[:, bass.ds(l + 1, 1), :].rearrange("p a n -> p (a n)"))\
                                .then_inc(cur_done, 1)
                        if t and not last:
                            low(m0 + TT + t - 1, t - 1)
                        if last:
                            dve.wait_ge(normed, m0 + TT + t + 1)
                            v.tensor_tensor(k.x_sb[:, t, :], k.x_sb[:, t, :], res[:, t, :], ALU.add)\
                                .then_inc(final_added, 1)

                over_layers(dve, body)

            @block.scalar
            def _(act):
                a = nc.scalar

                def weight_high(slot, st, n):
                    a.activation(wt_hi[:, slot, n, :], stage[st][:, n, :], ACT.Copy).then_inc(w_hi, 1)

                def high(m, t):
                    act.wait_ge(tp_ready, m + 1)
                    a.activation(xt_hi[:, :, t * P:(t + 1) * P], tp[t % 2][:], ACT.Copy).then_inc(xt_hi_done, 1)

                def tile_gelu(l, t):
                    act.wait_ge(tok_biased, 2 + 2 * TT * l + t + 1)
                    a.activation(pre[t % 2][:], pre[t % 2][:], ACT.Gelu_apprx_tanh).then_inc(tok_gelu, 1)

                for t in range(TT - 1):
                    high(t, t)
                act.sem_inc(w_hi, 32)
                act.sem_inc(f1_gelu, 4)

                def body(l):
                    last = is_last(l)
                    m0 = TT + 2 * TT * l

                    def chunk_piece(c, n):
                        if n == 0:
                            act.wait_ge(staged[stage_of(c)], 64 * l + 16 * (c // STAGES + 1))
                        weight_high(c, stage_of(c), n)

                    act.wait_ge(cur_done, l + 1)
                    for g in range(16):
                        if g == LAST_TILE:
                            high(m0 - 1, TT - 1)
                        which, at, half = GROUP_ORDER[g]
                        act.wait_ge(proj_ready, 24 * l + g + 1)
                        a.activation(relu_t[g % 2], half_of(bank(g)), ACT.Relu, scale=-1.0,
                                     bias=cur[:, NEG + 4 * which + at:NEG + 4 * which + at + 1]).then_inc(relu_done, 1)
                        act.wait_ge(relu_done, 16 * l + g + 1)
                        if g >= 2:
                            act.wait_ge(proj_used, 24 * l + g - 1)
                        a.activation(exp_t[g % 2][:], relu_t[g % 2], ACT.Exp, scale=-1.0).then_inc(exp_done, 1)
                        if g >= 4:
                            chunk_piece(F2 + (g - 4) // 4, g % 4)
                    for at in range(CH):
                        chunk_piece(F2 + 3, at)
                        act.wait_ge(kv_done, 4 * l + at + 1)
                        act.wait_ge(qz_done, 4 * l + at + 1)
                        a.activation(val_hi[:, at, :], qry_t[:, at, :], ACT.Copy,
                                     scale=kv[:, at:at + 1]).then_inc(val_hi_done, 1)
                    tile_gelu(l, 0)
                    tile_gelu(l, 1)
                    high(m0 + 0, 0)
                    high(m0 + 1, 1)
                    tile_gelu(l, 2)
                    tile_gelu(l, 3)

                    def hidden(j):
                        quarter, f = j // 4, j % FT
                        if j % 4 == 0 and quarter >= 2:
                            act.wait_ge(h_lo_done, 8 * l + quarter - 1)
                        act.wait_ge(f1_ready, 32 * l + j + 1)
                        a.activation(hf[quarter % 2][:, f % 4, :], mm[j % 4][:, 0:HALF], ACT.Gelu_apprx_tanh,
                                     bias=cur[:, BF1 + f:BF1 + f + 1]).then_inc(f1_gelu, 1)
                        if j % 4 == 3:
                            half, q = quarter // 4, quarter % 4
                            act.wait_ge(f1_gelu, 4 + 32 * l + j + 1)
                            a.activation(h_hi[:, 4 * q:4 * q + 4, half * HALF:(half + 1) * HALF], hf[quarter % 2][:],
                                         ACT.Copy).then_inc(h_hi_done, 1)
                            for n in range(2):
                                piece = 2 * quarter + n
                                if piece == 0:
                                    act.wait_ge(tok_ready, 2 * TT * l + TT)
                                chunk_piece(KQVO + piece // 4, piece % 4)

                    for j in range(32):
                        if j == 6:
                            high(m0 + 2, 2)
                        if j == 8:
                            high(m0 + 3, 3)
                        hidden(j)
                    for t in range(TT):
                        for n in range(4):
                            chunk_piece(F1 + t, n)
                        tile_gelu(l, TT + t)
                        if t and not last:
                            high(m0 + TT + t - 1, t - 1)

                over_layers(act, body)

            @block.tensor
            def _(pe):
                t_ = nc.tensor

                def transposes(m, t):
                    pe.wait_ge(normed, m + 1)
                    if not (isinstance(m, int) and m < 2):
                        pe.wait_ge(xt_lo_done, m - 1)
                    for c in range(CH):
                        x = t_.transpose(tp[t % 2][:, c, :], res[:, t, c * P:(c + 1) * P], k.ident[:])
                    x.then_inc(tp_ready, 1)

                for t in range(TT):
                    rows = slice(t * P, (t + 1) * P)
                    for c in range(PAIRS):
                        x = product3(t_, mm[t][:], (k.o_hi[:, c, rows], k.o_lo[:, c, rows]),
                                     (wt_hi[:, XWO, c, :], wt_lo[:, XWO, c, :]), c == 0, c == PAIRS - 1)
                    x.then_inc(projected, 1)
                pe.wait_ge(vec_in, 64)
                pe.wait_ge(zeroed, 1)
                t_.transpose(tp[0][:, 0, :], vec_rows[:, 0, :], k.ident[:])
                t_.transpose(tp[1][:, 0, :], vec_rows[:, 1, :], k.ident[:]).then_inc(cols_ready, 1)
                pe.wait_ge(cols_done, 4)
                for t in range(TT - 1):
                    transposes(t, t)

                def body(l):
                    last = is_last(l)
                    m0 = TT + 2 * TT * l

                    def project(out, chunk, at, first, count, ready=None):
                        toks, cols_ = slice(first * P, (first + count) * P), slice(at * P, (at + 1) * P)
                        out = half_of(out)[:, (first % 2) * P:(first % 2 + count) * P]
                        for c in range(CH):
                            x = product3(t_, out, (wt_hi[:, chunk, c, cols_], wt_lo[:, chunk, c, cols_]),
                                         (xt_hi[:, c, toks], xt_lo[:, c, toks]), c == 0, c == CH - 1)
                        if ready is not None:
                            x.then_inc(ready, 1)

                    pe.wait_ge(w_lo_dve, 32 * l + 16)
                    pe.wait_ge(xt_lo_done, m0 - 2)
                    pe.wait_ge(f1_gelu, 32 * l + 4)
                    for g in range(SECOND):
                        which, at, half = GROUP_ORDER[g]
                        project(bank(g), KQVO + which, at, 2 * half, 2, proj_ready)
                    pe.wait_ge(tok_biased, 2 * TT * l + 2)
                    pe.wait_ge(xt_lo_done, m0 - 1)
                    for g in range(SECOND, 8):
                        if g == 6:
                            transposes(m0 - 1, TT - 1)
                        if g == 7:
                            pe.wait_ge(proj_used, 24 * l + bank_freed(g))
                        project(bank(g), KQVO + K_, g - SECOND, 2, 1)
                    pe.wait_ge(xt_lo_done, m0)
                    for g in range(SECOND, 8):
                        project(bank(g), KQVO + K_, g - SECOND, 3, 1, proj_ready)
                    for g in range(8, 24):
                        which, at, half = GROUP_ORDER[g]
                        pe.wait_ge(proj_used, 24 * l + bank_freed(g))
                        project(bank(g), KQVO + which, at, 2 * half, 2, proj_ready)
                    def attention_out(t, c):
                        rows = slice(t * P, (t + 1) * P)
                        x = product3(t_, attn_out[t], (val_hi[:, c, rows], val_lo[:, c, rows]),
                                     (wt_hi[:, KQVO + 3, c, :], wt_lo[:, KQVO + 3, c, :]), c == 0, c == CH - 1)
                        if c == CH - 1:
                            x.then_inc(tok_ready, 1)

                    for c in range(CH):
                        pe.wait_ge(val_lo_done, 4 * l + c + 1)
                        for t in range(2):
                            attention_out(t, c)
                    pe.wait_ge(tok_biased, 2 * TT * l + 2)
                    for t in range(2, TT):
                        for c in range(CH):
                            attention_out(t, c)
                    transposes(m0 + 0, 0)
                    transposes(m0 + 1, 1)
                    pe.wait_ge(w_lo_dve, 32 * l + 32)
                    pe.wait_ge(proj_used, 24 * l + 24)
                    for t in range(2):
                        pe.wait_ge(xt_lo_done, m0 + t + 1)
                        for f in range(4):
                            project(mm[f], F1, f, t, 1, f1_ready if t else None)
                    for j in range(4, 32):
                        half, f = j // FT, j % FT
                        if j == 6:
                            transposes(m0 + 2, 2)
                        if j == 8:
                            transposes(m0 + 3, 3)
                        if j == FT:
                            pe.wait_ge(xt_lo_done, m0 + 4)
                        pe.wait_ge(f1_gelu, 32 * l + j + 1)
                        project(mm[j % 4], F1 + f // 4, f % 4, 2 * half, 2, f1_ready)
                    pe.wait_ge(w_lo_pool, 16 * l + 16)
                    for t in range(TT):
                        rows = slice(t * P, (t + 1) * P)
                        pe.wait_ge(tok_biased, 2 * TT * l + TT + t + 1)
                        pe.wait_ge(h_lo_done, 8 * l + (4 if t < 2 else 8))
                        for f in range(FT):
                            x = product3(t_, tok[t % 2][:], (h_hi[:, f, rows], h_lo[:, f, rows]),
                                         (wt_hi[:, F2 + f // 4, f % 4, :], wt_lo[:, F2 + f // 4, f % 4, :]),
                                         f == 0, f == FT - 1)
                        x.then_inc(tok_ready, 1)
                        if t and not last:
                            transposes(m0 + TT + t - 1, t - 1)

                over_layers(pe, body)


NE, ES, ESZ = 16, 4, 64
EX = NE * ES
GROUPS = TOK // NE
TILE_GROUPS = P // NE
EP = EX // 2
QUADS = EX * GROUPS // P
C_GROUP, C_HALF, C_TIE, C_COLS = 0, 8, 72, 88


def expert_phase(k):
    nc = k.nc
    with ExitStack() as ctx:
        def sb(name, shape, dt):
            return ctx.enter_context(nc.sbuf_tensor(name, shape, dt))

        def sem(name):
            return ctx.enter_context(nc.semaphore(name))

        def pb(name, shape, dt):
            return ctx.enter_context(nc.psum_tensor(name, shape, dt))

        wt_hi, wt_lo, f = k.wt_hi, k.wt_lo, k.res
        stage = [k.stage[:, n] for n in range(2)]
        cst = sb("cst", [P, C_COLS], F32)
        ctl = sb("ctl", [P, CH, EX], F32)
        ctl_hi = sb("ctl_hi", [P, CH, EX], F16)
        ctl_lo = sb("ctl_lo", [P, CH, EX], BF16)
        bias_rows = sb("bias_rows", [EP, P], F32)
        bias_cols = sb("bias_cols", [P, EP], F32)
        f_hi = sb("f_hi", [P, TT, D], F16)
        f_lo = sb("f_lo", [P, TT, D], BF16)
        ft_hi = sb("ft_hi", [P, CH, TOK], F16)
        ft_lo = sb("ft_lo", [P, CH, TOK], BF16)
        stats = sb("e_stats", [P, TT, 6], F32)
        mv = sb("e_mv", [P, TT, 2], F32)
        var_eps = sb("e_var_eps", [P, TT], F32)
        rstd = sb("e_rstd", [P, TT], F32)
        logits = k.stage[0:EX, 2, 2]
        top = sb("top", [EX, GROUPS], F32)
        pick_t = sb("pick_t", [EX, TOK], F16)
        pick = sb("pick", [P, TT, EX], F16)
        spread = sb("spread", [P, TT, EX, GROUPS], F16)
        sel_hi = sb("sel_hi", [P, CH, EX, GROUPS], F16)
        sel_lo = sb("sel_lo", [P, CH, EX, GROUPS], BF16)
        back = sel_hi[:].rearrange("p c e g -> p (c e g)").rearrange("p (q t) -> p q t", q=QUADS)
        inner = [k.stage[:, 2, n].rearrange("p (a n) -> p a n", a=8) for n in range(2)]
        in_hi = ft_hi[:].rearrange("p c n -> p (c n)").rearrange("p (a n) -> p a n", a=EP)
        in_lo = ft_lo[:].rearrange("p c n -> p (c n)").rearrange("p (a n) -> p a n", a=EP)
        it_hi = [f_hi[:, n, :] for n in range(2)]
        it_lo = [f_lo[:, n, :] for n in range(2)]
        work = [pb(f"e_work{n}", [P, D], F32) for n in range(4)]
        outs = [pb(f"e_out{n}", [P, D], F32) for n in range(TT)]

        c_in, staged = sem("e_c_in"), [sem(f"e_staged{n}") for n in range(2)]
        stats_done, mv_done, var_done, rstd_done, normed = (sem(n) for n in (
            "e_stats_done", "e_mv_done", "e_var_done", "e_rstd_done", "e_normed"))
        ctl_hi_done, ctl_lo_done, cleared, bias_ready, bias_done = (sem(n) for n in (
            "ctl_hi_done", "ctl_lo_done", "e_cleared", "bias_ready", "bias_done"))
        fr_hi_done, fr_lo_done, tp_ready, ft_hi_done, ft_lo_done = (sem(n) for n in (
            "fr_hi_done", "fr_lo_done", "e_tp_ready", "ft_hi_done", "ft_lo_done"))
        logits_ready, logits_done, top_done, pick_done, pick_ready, picks_done, spread_done = (sem(n) for n in (
            "logits_ready", "logits_done", "top_done", "pick_done", "pick_ready", "picks_done", "spread_done"))
        sel_ready, sel_hi_done, sel_lo_done = (sem(n) for n in ("sel_ready", "sel_hi_done", "sel_lo_done"))
        inner_ready, inner_biased, inner_relu, in_hi_done, in_lo_done = (sem(n) for n in (
            "inner_ready", "inner_biased", "inner_relu", "in_hi_done", "in_lo_done"))
        back_ready, back_done, inter_ready, it_hi_done, it_lo_done, out_ready, out_added, stored = (sem(n) for n in (
            "back_ready", "back_done", "inter_ready", "it_hi_done", "it_lo_done", "out_ready", "out_added", "e_stored"))
        given = sem("given")
        w_hi, w_lo_pool, w_lo_dve = sem("e_w_hi"), sem("e_w_lo_pool"), sem("e_w_lo_dve")

        def slot(m):
            return F2 + m if m < 4 else KQVO + m - 4

        with nc.Block() as block:
            @block.sync
            def _(sp):
                sp.dma_start(cst[:], k.expert_consts).then_inc(c_in, 16)
                sp.dma_start(ctl[:], k.controller.rearrange("(c p) n -> p c n", p=P)).then_inc(c_in, 16)
                sp.dma_start(bias_rows[:], k.ebias).then_inc(c_in, 16)
                for m in range(2):
                    sp.sem_inc(staged[m], 16)
                for m in range(2, 8):
                    if 2 <= m < 6:
                        sp.wait_ge(w_lo_pool, 4 * (m - 1))
                    elif m >= 6:
                        sp.wait_ge(w_lo_dve, 4 * (m - 5))
                    rows = k.ef2[m * D:(m + 1) * D, :].rearrange("(c p) n -> p c n", p=P)
                    sp.dma_start(stage[m % 2], rows).then_inc(staged[m % 2], 16)
                out_v = k.out.rearrange("(t p) d -> p t d", p=P)
                for t in range(TT):
                    sp.wait_ge(out_added, t + 1)
                    sp.dma_start(out_v[:, t, :], k.x_sb[:, t, :]).then_inc(stored, 16)
                sp.wait_ge(stored, 16 * TT)

            @block.gpsimd
            def _(pool):
                g = nc.gpsimd
                for t in range(TT):
                    pool.wait_ge(var_done, t + 1)
                    g.tensor_tensor(rstd[:, t:t + 1], var_eps[:, t:t + 1], k.neg_half[:, 0:1],
                                    ALU.pow).then_inc(rstd_done, 1)
                pool.wait_ge(rstd_done, TT)
                g.memset(spread[:], 0.0).then_inc(cleared, 1)
                pool.wait_ge(cleared, 1)
                for m in range(4):
                    pool.wait_ge(staged[m % 2], 16 * (m // 2 + 1))
                    for n in range(4):
                        pool.wait_ge(w_hi, 4 * m + n + 1)
                        g.tensor_tensor(wt_lo[:, slot(m), n, :], stage[m % 2][:, n, :], wt_hi[:, slot(m), n, :],
                                        ALU.subtract).then_inc(w_lo_pool, 1)

            @block.vector
            def _(dve):
                v = nc.vector
                for t in range(TT):
                    v.bn_stats(stats[:, t, :], k.x_sb[:, t, :]).then_inc(stats_done, 1)
                for t in range(TT):
                    dve.wait_ge(stats_done, t + 1)
                    v.bn_aggr(mv[:, t, :], stats[:, t, :]).then_inc(mv_done, 1)
                for t in range(TT):
                    dve.wait_ge(mv_done, t + 1)
                    v.tensor_scalar(var_eps[:, t:t + 1], mv[:, t, 1:2], EPS_OUTER, None, ALU.add).then_inc(var_done, 1)
                for t in range(TT):
                    dve.wait_ge(rstd_done, t + 1)
                    v.tensor_scalar(f[:, t, :], k.x_sb[:, t, :], mv[:, t, 0:1], rstd[:, t:t + 1],
                                    ALU.subtract, ALU.mult).then_inc(normed, 1)
                dve.wait_ge(c_in, 48)
                dve.wait_ge(ctl_hi_done, 1)
                v.tensor_tensor(ctl_lo[:], ctl[:], ctl_hi[:], ALU.subtract).then_inc(ctl_lo_done, 1)
                dve.wait_ge(bias_ready, 1)
                v.tensor_copy(bias_cols[:], work[3][:, 0:EP]).then_inc(bias_done, 1)
                for c in range(CH):
                    dve.wait_ge(ft_hi_done, c + 1)
                    v.tensor_tensor(ft_lo[:, c, :], work[c % 2][:], ft_hi[:, c, :], ALU.subtract).then_inc(ft_lo_done, 1)
                for t in range(TT):
                    dve.wait_ge(fr_hi_done, t + 1)
                    v.tensor_tensor(f_lo[:, t, :], f[:, t, :], f_hi[:, t, :], ALU.subtract).then_inc(fr_lo_done, 1)
                dve.wait_ge(logits_ready, 1)
                grouped = logits.rearrange("e (g t) -> e g t", t=NE)
                v.tensor_tensor(grouped, work[2][0:EX, :].rearrange("e (g t) -> e g t", t=NE),
                                cst[0:EX, C_TIE:C_TIE + NE].unsqueeze(1).to_broadcast([EX, GROUPS, NE]),
                                ALU.add).then_inc(logits_done, 1)
                dve.wait_ge(logits_done, 1)
                v.tensor_reduce(top[:], grouped, AX_X, ALU.max).then_inc(top_done, 1)
                dve.wait_ge(top_done, 1)
                v.tensor_tensor(pick_t[:].rearrange("e (g t) -> e g t", t=NE), grouped,
                                top[:].unsqueeze(2).to_broadcast([EX, GROUPS, NE]), ALU.is_equal).then_inc(pick_done, 1)
                dve.wait_ge(pick_ready, 1)
                v.tensor_copy(pick[:], work[3][:].bitcast(F16)[:, 0:TT * EX].rearrange("p (t e) -> p t e", t=TT))\
                    .then_inc(picks_done, 1)
                dve.wait_ge(picks_done, 1)
                dve.wait_ge(cleared, 1)
                for t in range(TT):
                    v.tensor_tensor(spread[:, t, :, t * TILE_GROUPS:(t + 1) * TILE_GROUPS],
                                    pick[:, t, :].unsqueeze(2).to_broadcast([P, EX, TILE_GROUPS]),
                                    cst[:, C_GROUP:C_GROUP + TILE_GROUPS].unsqueeze(1).to_broadcast([P, EX, TILE_GROUPS]),
                                    ALU.mult).then_inc(spread_done, 1)
                for n in range(TT * CH):
                    t, c = n // CH, n % CH
                    groups = slice(t * TILE_GROUPS, (t + 1) * TILE_GROUPS)
                    dve.wait_ge(sel_hi_done, n + 1)
                    v.tensor_tensor(sel_lo[:, c, :, groups], work[n % 4][:].rearrange("p (e g) -> p e g", g=TILE_GROUPS),
                                    sel_hi[:, c, :, groups], ALU.subtract).then_inc(sel_lo_done, 1)
                for b in range(EP // 8):
                    dve.wait_ge(inner_ready, 8 * (b + 1))
                    v.tensor_tensor(inner[b % 2], work[2 + b % 2][:].rearrange("p (a n) -> p a n", a=8),
                                    bias_cols[:, 8 * b:8 * b + 8].unsqueeze(2).to_broadcast([P, 8, 2 * GROUPS]),
                                    ALU.add).then_inc(inner_biased, 1)
                    dve.wait_ge(inner_biased, b + 1)
                    v.scalar_tensor_tensor(out=inner[b % 2], in0=inner[b % 2], scalar=0.0,
                                           in1=cst[:, C_HALF:C_HALF + 2 * GROUPS].unsqueeze(1).to_broadcast([P, 8, 2 * GROUPS]),
                                           op0=ALU.max, op1=ALU.mult).then_inc(inner_relu, 1)
                    dve.wait_ge(in_hi_done, b + 1)
                    v.tensor_tensor(in_lo[:, 8 * b:8 * b + 8, :], inner[b % 2], in_hi[:, 8 * b:8 * b + 8, :],
                                    ALU.subtract).then_inc(in_lo_done, 1)
                    dve.wait_ge(staged[b % 2], 16 * ((4 + b) // 2 + 1))
                    for n in range(4):
                        dve.wait_ge(w_hi, 16 + 4 * b + n + 1)
                        v.tensor_tensor(wt_lo[:, slot(4 + b), n, :], stage[b % 2][:, n, :], wt_hi[:, slot(4 + b), n, :],
                                        ALU.subtract).then_inc(w_lo_dve, 1)
                for q in range(QUADS):
                    dve.wait_ge(it_hi_done, q + 1)
                    v.tensor_tensor(it_lo[q % 2], work[q % 2][:], it_hi[q % 2], ALU.subtract).then_inc(it_lo_done, 1)
                for t in range(TT):
                    dve.wait_ge(out_ready, t + 1)
                    v.tensor_tensor(k.x_sb[:, t, :], k.x_sb[:, t, :], outs[t][:], ALU.add).then_inc(out_added, 1)

            @block.scalar
            def _(act):
                a = nc.scalar

                def weight_high(m):
                    act.wait_ge(staged[m % 2], 16 * (m // 2 + 1))
                    for n in range(4):
                        a.activation(wt_hi[:, slot(m), n, :], stage[m % 2][:, n, :], ACT.Copy).then_inc(w_hi, 1)

                weight_high(0)
                weight_high(1)
                act.wait_ge(c_in, 48)
                a.activation(ctl_hi[:], ctl[:], ACT.Copy).then_inc(ctl_hi_done, 1)
                for c in range(CH):
                    act.wait_ge(tp_ready, c + 1)
                    a.activation(ft_hi[:, c, :], work[c % 2][:], ACT.Copy).then_inc(ft_hi_done, 1)
                for t in range(TT):
                    a.activation(f_hi[:, t, :], f[:, t, :], ACT.Copy).then_inc(fr_hi_done, 1)
                for n in range(TT * CH):
                    t, c = n // CH, n % CH
                    act.wait_ge(sel_ready, n + 1)
                    a.activation(sel_hi[:, c, :, t * TILE_GROUPS:(t + 1) * TILE_GROUPS],
                                 work[n % 4][:].rearrange("p (e g) -> p e g", g=TILE_GROUPS), ACT.Copy).then_inc(sel_hi_done, 1)
                for m in range(2, 4):
                    weight_high(m)
                for b in range(EP // 8):
                    act.wait_ge(inner_relu, b + 1)
                    a.activation(in_hi[:, 8 * b:8 * b + 8, :], inner[b % 2], ACT.Copy).then_inc(in_hi_done, 1)
                    act.wait_ge(inner_ready, 4 * (b + 1))
                    weight_high(4 + b)
                for n in range(QUADS // 2):
                    act.wait_ge(back_ready, n + 1)
                    a.activation(back[:, 2 * n:2 * n + 2, :],
                                 work[2 + n % 2][:].bitcast(F16).rearrange("p (q t) -> p q t", q=2), ACT.Copy)\
                        .then_inc(back_done, 1)
                for q in range(QUADS):
                    act.wait_ge(inter_ready, q + 1)
                    if q >= 2:
                        act.wait_ge(given, q - 1)
                    a.activation(it_hi[q % 2], work[q % 2][:], ACT.Copy).then_inc(it_hi_done, 1)

            @block.tensor
            def _(pe):
                t_ = nc.tensor
                pe.wait_ge(c_in, 48)
                t_.transpose(work[3][:, 0:EP], bias_rows[:], k.ident[0:EP, 0:EP]).then_inc(bias_ready, 1)
                pe.wait_ge(normed, TT)
                for c in range(CH):
                    if c >= 2:
                        pe.wait_ge(ft_lo_done, c - 1)
                    for t in range(TT):
                        x = t_.transpose(work[c % 2][:, t * P:(t + 1) * P], f[:, t, c * P:(c + 1) * P], k.ident[:])
                    x.then_inc(tp_ready, 1)
                pe.wait_ge(ft_lo_done, CH)
                pe.wait_ge(ctl_lo_done, 1)
                for c in range(CH):
                    x = product3(t_, work[2][0:EX, :], (ctl_hi[:, c, :], ctl_lo[:, c, :]),
                                 (ft_hi[:, c, :], ft_lo[:, c, :]), c == 0, c == CH - 1)
                x.then_inc(logits_ready, 1)
                pe.wait_ge(pick_done, 1)
                pe.wait_ge(bias_done, 1)
                picks = work[3][:].bitcast(F16)
                for t in range(TT):
                    x = t_.transpose(picks[:, t * EX:(t + 1) * EX], pick_t[:, t * P:(t + 1) * P], k.ident16[0:EX, 0:EX])
                x.then_inc(pick_ready, 1)
                pe.wait_ge(fr_lo_done, TT)
                for n in range(TT * CH):
                    t, c = n // CH, n % CH
                    if c == 0:
                        pe.wait_ge(spread_done, t + 1)
                    if n >= 4:
                        pe.wait_ge(sel_lo_done, n - 3)
                    rhs = spread[:, t, :, t * TILE_GROUPS:(t + 1) * TILE_GROUPS]
                    out = work[n % 4][:].rearrange("p (e g) -> p e g", g=TILE_GROUPS)
                    t_.matmul(out, f_hi[:, t, c * P:(c + 1) * P], rhs, start=True, stop=False)
                    t_.matmul(out, f_lo[:, t, c * P:(c + 1) * P], rhs, start=False, stop=True).then_inc(sel_ready, 1)
                pe.wait_ge(sel_lo_done, TT * CH)
                for q in range(EP):
                    b = q // 8
                    if q % 8 == 0 and b >= 2:
                        pe.wait_ge(inner_biased, b - 1)
                    out = work[2 + b % 2][:, (q % 8) * 2 * GROUPS:(q % 8 + 1) * 2 * GROUPS]
                    cols_ = slice((q % 4) * P, (q % 4 + 1) * P)
                    for c in range(CH):
                        x = product3(t_, out, (wt_hi[:, KQVO + q // 4, c, cols_], wt_lo[:, KQVO + q // 4, c, cols_]),
                                     (sel_hi[:, c, 2 * q:2 * q + 2, :], sel_lo[:, c, 2 * q:2 * q + 2, :]),
                                     c == 0, c == CH - 1)
                    x.then_inc(inner_ready, 1)
                pe.wait_ge(inner_biased, EP // 8)
                for n in range(QUADS // 2):
                    if n >= 2:
                        pe.wait_ge(back_done, n - 1)
                    out = work[2 + n % 2][:].bitcast(F16)
                    for q in range(2):
                        for t in range(TT):
                            e = 4 * (2 * n + q)
                            x = t_.transpose(out[:, q * TOK + t * P:q * TOK + (t + 1) * P],
                                             spread[:, t, e:e + 4, :].rearrange("p e g -> p (e g)"), k.ident16[:])
                    x.then_inc(back_ready, 1)

                def expert_out(q):
                    if q >= 2:
                        pe.wait_ge(it_lo_done, q - 1)
                    for half in range(2):
                        pair = 2 * q + half
                        m, n = slot(pair // 4), pair % 4
                        x = product3(t_, work[q % 2][half * 64:(half + 1) * 64, :], (in_hi[:, pair, :], in_lo[:, pair, :]),
                                     (wt_hi[:, m, n, :], wt_lo[:, m, n, :]), True, True)
                    x.then_inc(inter_ready, 1)

                def give_back(q):
                    pe.wait_ge(it_lo_done, q + 1)
                    for t in range(TT):
                        lhs = back[:, q, t * P:(t + 1) * P]
                        t_.matmul(outs[t][:], lhs, it_hi[q % 2], start=q == 0, stop=False)
                        x = t_.matmul(outs[t][:], lhs, it_lo[q % 2], start=False, stop=q == QUADS - 1)
                        if q == QUADS - 1:
                            x.then_inc(out_ready, 1)
                        elif t == TT - 1:
                            x.then_inc(given, 1)

                pe.wait_ge(in_lo_done, EP // 8)
                pe.wait_ge(w_lo_pool, 16)
                pe.wait_ge(back_done, QUADS // 2)
                for q in range(QUADS + 1):
                    if q == QUADS // 2:
                        pe.wait_ge(w_lo_dve, 16)
                    if q < QUADS:
                        expert_out(q)
                    if q:
                        give_back(q - 1)


def perceiver_kernel(nc, args, out):
    k = Kernel()
    k.nc = nc
    k.out = out.rearrange("a t d -> (a t) d")
    k.x = args["x"].rearrange("a t d -> (a t) d")
    k.ctx = args["ctx_1024"].rearrange("a t d -> (a t) d")
    k.rope = args["rope"]
    k.gamma_x, k.beta_x = args["L0_xattn_gamma_x"], args["L0_xattn_beta_x"]
    k.gamma_l, k.beta_l = args["L0_xattn_gamma_l"], args["L0_xattn_beta_l"]
    k.wq, k.wkv, k.xwo = args["L0_xattn_Wq"], args["L0_xattn_Wkv"], args["L0_xattn_Wo"]
    a = {n.removeprefix("L0_attn_"): v for n, v in args.items() if n.startswith("L0_attn_")}
    k.wq_l, k.bq, k.wk, k.bk, k.wv, k.bv, k.wo, k.bo = (a[n] for n in ("Wq", "bq", "Wk", "bk", "Wv", "bv", "Wo", "bo"))
    k.ln1_s, k.ln1_b, k.ln2_s, k.ln2_b = (a[n] for n in ("ln1_s", "ln1_b", "ln2_s", "ln2_b"))
    k.wf1, k.bf1, k.wf2, k.bf2 = (a[n] for n in ("Wf1", "bf1", "Wf2", "bf2"))
    k.ef1 = args["L0_ffn_f1"].rearrange("d e s f -> d (e s f)")
    k.ef2 = args["L0_ffn_f2"].rearrange("e s f d -> (e s f) d")
    k.ebias = args["L0_ffn_bias"].rearrange("e s f -> (e s f)").rearrange("(q n) -> q n", n=P)
    k.controller = args["L0_ffn_controller"].rearrange("d e s -> d (e s)")
    k.expert_consts = args["expert_consts"]
    k.keys = nc.dram_tensor("keys", (2, BLOCKS, P, BLK), F16, kind="Internal").ap()
    k.values = nc.dram_tensor("values", (BLOCKS, P, SUB, P), F32, kind="Internal").ap()
    keys_v = k.keys.rearrange("l (a b) q n -> l b q a n", a=PAIRS)
    values_v = k.values.rearrange("(a b) p t c -> b p a t c", a=PAIRS)
    k.k_store = lambda hl, b: keys_v[hl, b]
    k.v_store = lambda b: values_v[b]
    with ExitStack() as ctx:
        def sb(name, shape, dt):
            return ctx.enter_context(nc.sbuf_tensor(name, shape, dt))

        k.x_sb = sb("x_sb", [P, TT, D], F32)
        k.ident = sb("ident", [P, P], F32)
        k.ident16 = sb("ident16", [P, P], F16)
        k.ones = sb("ones", [P, P], F32)
        k.neg_half = sb("neg_half", [P, 16], F32)
        k.res = sb("res", [P, TT, D], F32)
        k.wt_hi = sb("wt_hi", [P, CHUNKS, 4, D], F16)
        k.wt_lo = sb("wt_lo", [P, CHUNKS, 4, D], BF16)
        k.stage = sb("stage", [P, STAGES, 4, D], F32)
        with nc.sbuf_tensor("h_lo", [P, FT, TOK], BF16) as k.h_lo, ExitStack() as xattn:
            def xsb(name, shape, dt):
                return xattn.enter_context(nc.sbuf_tensor(name, shape, dt))
            k.o_hi, k.o_lo = k.h_lo[:, 0:PAIRS].bitcast(F16), k.h_lo[:, PAIRS:2 * PAIRS]
            k.q_hi = xsb("q_hi", [P, 2 * PAIRS, TOK], F16)
            k.q_lo = xsb("q_lo", [HD + 1, 2 * PAIRS, TOK], F16)
            k.wg_hi, k.wg_lo = slots(k.wt_hi, 0, 2, F16, 2 * D), slots(k.wt_lo, 0, 2, BF16, 2 * D)
            k.kt = [k.wt_hi[:, 4 - 2 * u:6 - 2 * u] for u in range(2)]
            k.pmax = xsb("pmax", [P, UNITS, KB], F32)
            k.kv_bias = slots(k.wt_lo, 8, 1, F32, 2 * D)[:, 0]
            latents_phase(k)
            context_phase(k)
            attention_phase(k)
            xattn.close()
            layers_phase(k)
        expert_phase(k)


_INS = ["x", "ctx_1024", "L0_xattn_gamma_x", "L0_xattn_beta_x", "L0_xattn_gamma_l", "L0_xattn_beta_l",
        "L0_xattn_Wq", "L0_xattn_Wkv", "L0_xattn_Wo",
        "L0_attn_Wq", "L0_attn_bq", "L0_attn_Wk", "L0_attn_bk", "L0_attn_Wv", "L0_attn_bv", "L0_attn_Wo",
        "L0_attn_bo", "L0_attn_ln1_s", "L0_attn_ln1_b", "L0_attn_Wf1", "L0_attn_bf1", "L0_attn_Wf2",
        "L0_attn_bf2", "L0_attn_ln2_s", "L0_attn_ln2_b",
        "L0_ffn_controller", "L0_ffn_f1", "L0_ffn_f2", "L0_ffn_bias"]


def rope_table():
    exponent = np.arange(0, HD, 2, dtype=np.float32) / np.float32(HD)
    inv_freq = (np.float32(1.0) / np.power(np.float32(10000.0), exponent)).astype(np.float32)
    theta = np.arange(CTX, dtype=np.float32)[:, None] * inv_freq[None, :]
    table = np.concatenate([np.cos(theta), np.sin(theta)], axis=1).astype(np.float32)
    return np.ascontiguousarray(table.reshape(CTX // P, P, HD).transpose(1, 0, 2))


def expert_table():
    table = np.zeros((P, C_COLS), np.float32)
    row = np.arange(P)
    table[row, C_GROUP + row // NE] = 1.0
    table[:, C_HALF:C_HALF + 2 * GROUPS] = (row[:, None] // ESZ) == (np.arange(2 * GROUPS)[None, :] // GROUPS)
    table[:, C_TIE:C_TIE + NE] = np.linspace(0.0, 1e-6, NE, dtype=np.float32)
    return table


def kernel(**inputs):
    import numpy as _np
    import concourse.bacc as _bacc
    from concourse import mybir as _mybir
    from concourse.bass_utils import run_bass_kernel_spmd as _run

    nc = _bacc.Bacc("TRN2", target_bir_lowering=False, num_devices=1)
    arrays, args = {}, {}
    for name, a in [(n, inputs[n]) for n in _INS] + [("rope", rope_table()), ("expert_consts", expert_table())]:
        a = _np.ascontiguousarray(a)
        arrays[f"in_{name}"] = a
        args[name] = nc.dram_tensor(f"in_{name}", a.shape, _mybir.dt.from_np(a.dtype), kind="ExternalInput").ap()
    out = nc.dram_tensor("out_0", (1, TOK, D), _mybir.dt.float32, kind="ExternalOutput").ap()
    perceiver_kernel(nc, args, out)
    r = _run(nc, [arrays], core_ids=[0])
    return r.results[0]["out_0"]
```
